# Optimizing a Trainium2 kernel written in Bass

```python
import numpy as np
import jax
import jax.numpy as jnp

def _softmax(x, axis=-1):
    return jax.nn.softmax(x, axis=axis)

def _gelu(x):
    return jax.nn.gelu(x, approximate=True)

def _silu(x):
    return jax.nn.silu(x)

def _sigmoid(x):
    return jax.nn.sigmoid(x)

def _layernorm(x, axis=-1, eps=1e-05):
    m = jnp.mean(x, axis=axis, keepdims=True)
    v = jnp.var(x, axis=axis, keepdims=True)
    return (x - m) / jnp.sqrt(v + eps)

def _scatter_add(tgt, idx, src, axis=0):
    return tgt.at[idx].add(src)

def _segment_sum(src, seg, n):
    return jax.ops.segment_sum(src, seg, n)
kernel_name = 'mk_prb_d1_jaxref_r8_6be1d0'

def setup_inputs(seed: int=0):
    np.random.seed(seed)
    _w = jnp.asarray

    def _L0_attn_setup():
        import jax, jax.numpy as jnp
        import numpy as np
        import math
        HIDDEN = 128
        HEADS = 16
        HEAD_DIM = HIDDEN // HEADS
        B, S = (2, 256)

        def _xavier(key, shape):
            fan_in, fan_out = (shape[1], shape[0])
            limit = math.sqrt(6.0 / (fan_in + fan_out))
            return jax.random.uniform(key, shape, jnp.float32, -limit, limit)
        key = jax.random.key(seed)
        ks = jax.random.split(key, 5)
        x = jax.random.normal(ks[0], (B, S, HIDDEN), jnp.float32)
        Wq = _xavier(ks[1], (HIDDEN, HIDDEN))
        Wk = _xavier(ks[2], (HIDDEN, HIDDEN))
        Wv = _xavier(ks[3], (HIDDEN, HIDDEN))
        Wo = _xavier(ks[4], (HIDDEN, HIDDEN))
        bq = jnp.zeros((HIDDEN,), jnp.float32)
        bk = jnp.zeros((HIDDEN,), jnp.float32)
        bv = jnp.zeros((HIDDEN,), jnp.float32)
        bo = jnp.zeros((HIDDEN,), jnp.float32)
        return {'x': x, 'Wq': Wq, 'bq': bq, 'Wk': Wk, 'bk': bk, 'Wv': Wv, 'bv': bv, 'Wo': Wo, 'bo': bo}
    _L0_attn_in = _L0_attn_setup()

    def _L0_ffn_setup():
        import jax, jax.numpy as jnp
        import numpy as np
        key = jax.random.key(seed)
        k1, k2, k3 = jax.random.split(key, 3)
        B, T, D, E = (4, 256, 128, 8)
        x = jax.random.normal(k1, (B, T, D), dtype=jnp.float32)
        gate_w = jax.random.normal(k2, (E, D), dtype=jnp.float32) * (1.0 / np.sqrt(D))
        bound = float(np.sqrt(6.0 / (D + D)))
        We = jax.random.uniform(k3, (E, D, D), dtype=jnp.float32, minval=-bound, maxval=bound)
        return {'x': x, 'gate_w': gate_w, 'We': We}
    _L0_ffn_in = _L0_ffn_setup()
    _d = {'L0_attn_x': _L0_attn_in['x'], 'L0_attn_Wq': _L0_attn_in['Wq'], 'L0_attn_bq': _L0_attn_in['bq'], 'L0_attn_Wk': _L0_attn_in['Wk'], 'L0_attn_bk': _L0_attn_in['bk'], 'L0_attn_Wv': _L0_attn_in['Wv'], 'L0_attn_bv': _L0_attn_in['bv'], 'L0_attn_Wo': _L0_attn_in['Wo'], 'L0_attn_bo': _L0_attn_in['bo'], 'L0_ffn_gate_w': _L0_ffn_in['gate_w'], 'L0_ffn_We': _L0_ffn_in['We']}
    _x0 = _d['L0_attn_x']
    _d['L0_attn_x'] = jax.random.normal(jax.random.fold_in(jax.random.key(seed), 1), (32, 256, 128), dtype=_x0.dtype)
    del _x0
    return _d

def reference(L0_attn_x, L0_attn_Wq, L0_attn_bq, L0_attn_Wk, L0_attn_bk, L0_attn_Wv, L0_attn_bv, L0_attn_Wo, L0_attn_bo, L0_ffn_gate_w, L0_ffn_We):

    def _L0_attn_ref(x, Wq, bq, Wk, bk, Wv, bv, Wo, bo):
        import jax, jax.numpy as jnp
        import numpy as np
        import math
        HIDDEN = 128
        HEADS = 16
        HEAD_DIM = HIDDEN // HEADS
        B, S = (2, 256)

        def _xavier(key, shape):
            fan_in, fan_out = (shape[1], shape[0])
            limit = math.sqrt(6.0 / (fan_in + fan_out))
            return jax.random.uniform(key, shape, jnp.float32, -limit, limit)
        b, s, d = x.shape
        h, hd = (HEADS, HEAD_DIM)
        q = (x @ Wq.T + bq).reshape(b, s, h, hd).transpose(0, 2, 1, 3)
        k = (x @ Wk.T + bk).reshape(b, s, h, hd).transpose(0, 2, 1, 3)
        v = (x @ Wv.T + bv).reshape(b, s, h, hd).transpose(0, 2, 1, 3)
        scores = jnp.einsum('bhqd,bhkd->bhqk', q, k) / math.sqrt(hd)
        causal = jnp.tril(jnp.ones((s, s), bool))
        scores = jnp.where(causal, scores, -jnp.inf)
        attn = jax.nn.softmax(scores, axis=-1)
        out = jnp.einsum('bhqk,bhkd->bhqd', attn, v)
        out = out.transpose(0, 2, 1, 3).reshape(b, s, d)
        return out @ Wo.T + bo

    def _L0_ffn_ref(x, gate_w, We):
        import jax, jax.numpy as jnp
        import numpy as np
        top_k = 2
        logits = jnp.einsum('btd,ed->bte', x, gate_w)
        top_val, top_idx = jax.lax.top_k(logits, top_k)
        top_w = jax.nn.softmax(top_val, axis=-1)
        y_all = jnp.einsum('btd,edm->btem', x, We)
        x_experts = jnp.take_along_axis(y_all, top_idx[..., None], axis=2)
        out = jnp.sum(x_experts * top_w[..., None], axis=2)
        return out
    x = L0_attn_x
    xn = _layernorm(x, axis=-1)
    x = x + _L0_attn_ref(xn, L0_attn_Wq, L0_attn_bq, L0_attn_Wk, L0_attn_bk, L0_attn_Wv, L0_attn_bv, L0_attn_Wo, L0_attn_bo) + _L0_ffn_ref(xn, L0_ffn_gate_w, L0_ffn_We)
    return x

_drawn_inputs = setup_inputs


def setup_inputs(seed=0):
    import zlib

    import numpy as np

    out = dict(_drawn_inputs(seed))
    spreads = {'L0_attn_bq': (0.0, 0.582),
     'L0_attn_bk': (0.0, 0.8),
     'L0_attn_bv': (0.0, 0.1),
     'L0_attn_bo': (0.0, 0.1)}
    factors = {}
    for name, (base, spread) in spreads.items():
        noise = np.random.default_rng([zlib.crc32(name.encode()), seed]).standard_normal(out[name].shape)
        drawn = base * np.exp(spread * noise) if base else spread * noise
        out[name] = jnp.asarray(drawn.astype(out[name].dtype))
    for name, factor in factors.items():
        out[name] = (out[name] * factor).astype(out[name].dtype)
    return out
```

```python
from contextlib import ExitStack

import concourse.bass as bass
from concourse import mybir

FP32 = mybir.dt.float32
BF16 = mybir.dt.bfloat16
U32 = mybir.dt.uint32
ALU = mybir.AluOpType
ACT = mybir.ActivationFunctionType
AX = mybir.AxisListType

NSEQ, S, D = 32, 256, 128
H, HD = 16, 8
E = 8
P = 128
QT = S // P
PARTS = 3
SLOT_ROWS = PARTS * HD
PROD_ROWS = PARTS * SLOT_ROWS
MAX_ROW = 96
ALL_ROWS = MAX_ROW + PARTS
HG = 4
NG = H // HG
ITEMS = 3 * NG
VW = 32
VGRP = 3
OW = HD + 1
VG = D + E
EH = 4
SCALE = float(HD) ** -0.5
EPS = 1e-5
MASKED = -3.0e38


def stand_alone(eng, passed):
    eng.sem_inc(passed, 1)


class Seq:

    def __init__(self, i, c):
        self.i, self.c = i, c

    def __add__(self, k):
        return Seq(self.i, self.c + k)

    @property
    def n(self):
        return self.i * 2 + self.c

    @property
    def par(self):
        return self.c % 2

    @property
    def half(self):
        return self.i + self.c // 2

    @property
    def static(self):
        return isinstance(self.i, int)


def wait(eng, sem, seq, per=1, k=None, unit=1):
    if seq.static and seq.n < 0:
        return
    k = per if k is None else k
    if seq.static and per * seq.n + k <= 0:
        return
    eng.wait_ge(sem, (seq.n * per + k) * unit)


def wait_half(eng, sem, seq, unit=16):
    if seq.static and seq.n < 0:
        return
    eng.wait_ge(sem, (seq.half + 1) * unit)


def bass_block(nc, x, wq, wk, bq, bk, wv, bv, wo, bo, gate, we, out):
    ctx = ExitStack()
    with ctx:
        def sb(name, shape, dt=FP32):
            return ctx.enter_context(nc.sbuf_tensor(name, shape, dt))

        def pb(name):
            return ctx.enter_context(nc.psum_tensor(name, [P, 512], FP32))

        def sem(name):
            return ctx.enter_context(nc.semaphore(name))

        wqk_sb = sb("wqk_sb", [P, 2, D])
        bqk_sb = sb("bqk_sb", [P, 2])
        wvg_sb = sb("wvg_sb", [P, VG])
        wo_sb = sb("wo_sb", [P, D])
        we_sb = sb("we_sb", [P, E, D])
        bv_sb = sb("bv_sb", [P, 1])
        bv_wide = sb("bv_wide", [P, P])
        bias_out = sb("bias_out", [P, D])
        ident = sb("ident", [P, P])
        ident_b = sb("ident_b", [P, P], BF16)
        mask_b = sb("mask_b", [P, P], BF16)
        expert_no = sb("expert_no", [P, E])
        minus_half = sb("minus_half", [P, QT])
        x_sb = [sb(f"x_sb{b}", [P, QT, D]) for b in range(2)]
        xb = [sb(f"xb{b}", [P, QT, D]) for b in range(2)]
        xnT = [sb(f"xnT{b}", [P, S]) for b in range(2)]
        qstack = [sb(f"qstack{b}", [P, H, S], BF16) for b in range(2)]
        kstack = [sb(f"kstack{b}", [P, H, S], BF16) for b in range(2)]
        vaug = [sb(f"vaug{b}", [P, QT, H, VW]) for b in range(2)]
        res = [sb(f"res{b}", [P, QT, D]) for b in range(2)]
        out_sb = [sb(f"out_sb{b}", [P, QT, D]) for b in range(2)]
        probs = [sb(f"probs{b}", [P, 3, HG, P]) for b in range(2)]
        stats = sb("stats", [P, QT, 6])
        mv = sb("mv", [P, QT, 2])
        var_eps = sb("var_eps", [P, QT])
        rstd = sb("rstd", [P, QT])
        xn = sb("xn", [P, QT, D])
        parts = sb("parts", [P, 2, PARTS, S], BF16)
        rest = sb("rest", [P, 2, S])
        negmax = sb("negmax", [P, QT, H])
        mrest = sb("mrest", [P, QT, H])
        mparts = sb("mparts", [P, QT, PARTS, H], BF16)
        mT = sb("mT", [PARTS * H, S], BF16)
        logits = sb("logits", [P, QT, E])
        top = sb("top", [P, QT, 8])
        topi = sb("topi", [P, QT, 8], U32)
        topf = sb("topf", [P, QT, 2])
        gap = sb("gap", [P, QT])
        egap = sb("egap", [P, QT])
        egap1 = sb("egap1", [P, QT])
        gw = sb("gw", [P, 2, QT])
        pick = sb("pick", [P, 2, QT, E])
        weight = sb("weight", [P, QT, E])
        oT = sb("oT", [P, 2, S])
        rden = sb("rden", [P, QT, H])
        o_sb = sb("o_sb", [P, QT, D])
        oTn = sb("oTn", [P, S])

        score_ps = [pb(f"score_ps{b}") for b in range(2)]
        scoreT_ps = [pb(f"scoreT_ps{b}") for b in range(2)]
        oT_ps = pb("oT_ps")
        m0, m1, m2 = pb("m0"), pb("m1"), pb("m2")
        moe_ps = [m1, m2]

        scratch = [nc.dram_tensor(f"scratch{b}", [2 * PARTS, P, S], BF16, kind="Internal").ap() for b in range(2)]

        ld_w = sem("ld_w")
        ld_bias = sem("ld_bias")
        pool_const = sem("pool_const")
        dve_const = sem("dve_const")
        pe_bias = sem("pe_bias")
        dve_bias = sem("dve_bias")
        dma_x = [sem(f"dma_x{b}") for b in range(2)]
        dma_scratch = sem("dma_scratch")
        dma_stack = sem("dma_stack")
        dma_max = sem("dma_max")
        dma_out = [sem(f"dma_out{b}") for b in range(2)]
        dve_stats, pool_eps, pool_rstd, pool_xb, dve_xn = (sem(n) for n in ("dve_stats", "pool_eps", "pool_rstd", "pool_xb", "dve_xn"))
        pe_xnT, act_xnT = sem("pe_xnT"), sem("act_xnT")
        pe_qk, act_part1, dve_rest, act_part2, pool_part3 = (sem(n) for n in ("pe_qk", "act_part1", "dve_rest", "act_part2", "pool_part3"))
        pe_score, dve_max, dve_mparts, pe_mT, act_mT = (sem(n) for n in ("pe_score", "dve_max", "dve_mparts", "pe_mT", "act_mT"))
        pe_vg, act_v, dve_logits, dve_gap, act_gate, dve_weight = (sem(n) for n in ("pe_vg", "act_v", "dve_logits", "dve_gap", "act_gate", "dve_weight"))
        pe_scoreT, act_exp, pool_mask, pe_pv, act_oT = (sem(n) for n in ("pe_scoreT", "act_exp", "pool_mask", "pe_pv", "act_oT"))
        pe_moe, dve_moe = sem("pe_moe"), sem("dve_moe")
        pe_o, dve_o, pe_oTn, act_oTn, pe_y, dve_out = (sem(n) for n in ("pe_o", "dve_o", "pe_oTn", "act_oTn", "pe_y", "dve_out"))
        dve_step = sem("dve_step")
        pool_passed, dve_passed, pe_passed = (sem(n) for n in ("pool_passed", "dve_passed", "pe_passed"))

        NSTACK = 8
        NW = 9
        LOOP0, LOOPS = 2, 14

        x_t = x.rearrange("(s q p) d -> s p q d", q=QT, p=P)
        out_t = out.rearrange("(s q p) d -> s p q d", q=QT, p=P)

        def over_slots(eng_fori, slot):
            for s in range(-1, LOOP0):
                slot(Seq(0, s), s)
            with eng_fori(0, LOOPS) as i:
                for u in range(2):
                    slot(Seq(i, LOOP0 + u), LOOP0 + u)
            for s in range(LOOP0 + 2 * LOOPS, NSEQ + 1):
                slot(Seq(0, s), s)

        def prepares(s):
            return s + 1 < NSEQ

        def scores(s):
            return 0 <= s < NSEQ

        def finishes(s):
            return 1 <= s

        block = ctx.enter_context(nc.Block())

        @block.sync
        def _(sp):
            sp.dma_start(x_sb[0][:], x_t[0]).then_inc(dma_x[0], 16)
            sp.dma_start(wqk_sb[:, 0, :], wq).then_inc(ld_w, 16)
            sp.dma_start(wqk_sb[:, 1, :], wk).then_inc(ld_w, 16)
            sp.dma_start(bqk_sb[:, 0:1], bq.unsqueeze(1)).then_inc(ld_w, 16)
            sp.dma_start(bqk_sb[:, 1:2], bk.unsqueeze(1)).then_inc(ld_w, 16)
            sp.dma_start(wvg_sb[:, 0:D], wv).then_inc(ld_w, 16)
            sp.dma_start(wvg_sb[:, D:VG], gate).then_inc(ld_w, 16)
            sp.dma_start(wo_sb[:], wo).then_inc(ld_w, 16)
            sp.dma_start(bv_sb[:], bv.unsqueeze(1)).then_inc(ld_w, 16)
            sp.dma_start(we_sb[:], we.rearrange("e d m -> d e m")).then_inc(ld_w, 16)
            sp.dma_start(bias_out[:], bo.unsqueeze(0).to_broadcast([P, D])).then_inc(ld_bias, 16)

            def slot(t, s):
                pre, fin = t + 1, t + (-1)
                if finishes(s - 1):
                    prev = fin + (-1)
                    wait(sp, dve_out, prev)
                    sp.dma_start(out_t[prev.n], out_sb[prev.par][:]).then_inc(dma_out[prev.par], 16)
                if prepares(s + 1):
                    nxt = pre + 1
                    wait(sp, dve_xn, nxt + (-2))
                    wait(sp, pool_xb, nxt + (-2))
                    sp.dma_start(x_sb[nxt.par][:], x_t[nxt.n]).then_inc(dma_x[nxt.par], 16)
                if prepares(s):
                    wait(sp, act_part1, pre)
                    wait(sp, act_part2, pre)
                    wait(sp, pool_part3, pre)
                    scr = scratch[pre.par]
                    sp.dma_start(scr.rearrange("a r t -> r a t"),
                                 parts[:].rearrange("p a b t -> p (a b) t")).then_inc(dma_scratch, 16)
                    wait(sp, dma_scratch, pre, unit=16)
                    wait(sp, pe_scoreT, fin, per=ITEMS)
                    wait(sp, pe_score, fin, per=ITEMS)
                    if s == -1:
                        sp.wait_ge(dve_const, 1)
                    rows = scr.rearrange("a (d h) t -> (a d) (h t)", h=H)
                    qs, ks = (st[pre.par][:].rearrange("p h t -> p (h t)") for st in (qstack, kstack))
                    for r in range(PARTS):
                        a, b = r * SLOT_ROWS, (PARTS - r) * HD
                        sp.dma_start(qs[a:a + SLOT_ROWS], rows[0:SLOT_ROWS]).then_inc(dma_stack, 16)
                        sp.dma_start(ks[a:a + b], rows[SLOT_ROWS + r * HD:2 * SLOT_ROWS]).then_inc(dma_stack, 16)
                        if r:
                            sp.dma_start(ks[a + b:a + SLOT_ROWS], rows[SLOT_ROWS:SLOT_ROWS + r * HD]).then_inc(dma_stack, 16)

            over_slots(sp.Fori, slot)
            last = Seq(0, NSEQ - 1)
            wait(sp, dve_out, last)
            sp.dma_start(out_t[last.n], out_sb[last.par][:]).then_inc(dma_out[last.par], 16)
            for b in range(2):
                sp.wait_ge(dma_out[b], 16 * (NSEQ // 2))

        @block.gpsimd
        def _(pool):
            g = nc.gpsimd
            g.memset(minus_half[:], -0.5).then_inc(pool_const, 1)
            g.memset(ident[:], 0.0).then_inc(pool_const, 1)
            g.memset(ident_b[:], 0.0).then_inc(pool_const, 1)
            g.memset(mask_b[:], 0.0).then_inc(pool_const, 1)
            g.iota(expert_no[:], pattern=[[1, E]], base=0, channel_multiplier=0,
                   allow_small_or_imprecise_dtypes=True).then_inc(pool_const, 1)
            pool.wait_ge(pool_const, 5)
            for m in (ident, ident_b):
                g.affine_select(out=m[:], in_=m[:], compare_op=ALU.not_equal, fill=1.0, base=0,
                                pattern=[[-1, P]], channel_multiplier=1).then_inc(pool_const, 1)
            g.affine_select(out=mask_b[:], in_=mask_b[:], compare_op=ALU.is_ge, fill=MASKED, base=0,
                            pattern=[[-1, P]], channel_multiplier=1).then_inc(pool_const, 1)

            def rstd_of(n):
                wait(pool, dve_stats, n)
                wait(pool, dve_xn, n + (-1))
                stand_alone(pool, pool_passed)
                g.tensor_scalar(var_eps[:], mv[:, :, 1], 1.0, EPS, ALU.mult, ALU.add).then_inc(pool_eps, 1)
                wait(pool, pool_eps, n)
                g.tensor_tensor(rstd[:], var_eps[:], minus_half[:], ALU.pow).then_inc(pool_rstd, 1)

            def slot(t, s):
                pre, fin = t + 1, t + (-1)
                for grp in range(NG):
                    if finishes(s):
                        k = 3 * (grp + 1)
                        wait(pool, act_exp, fin, per=ITEMS, k=k)
                        stand_alone(pool, pool_passed)
                        both = probs[grp % 2][:, 0:2].rearrange("p b h c -> p (b h) c")
                        g.affine_select(out=both, in_=both, compare_op=ALU.is_ge, fill=0.0, base=0,
                                        pattern=[[0, 2 * HG], [1, P]], channel_multiplier=-1).then_inc(pool_mask, 1)
                    if prepares(s) and grp == 1:
                        wait_half(pool, dma_x[pre.par], pre)
                        wait(pool, dve_moe, pre + (-2), per=4)
                        if s == -1:
                            pool.wait_ge(dve_bias, 1)
                        g.tensor_tensor(xb[pre.par][:], x_sb[pre.par][:],
                                        bias_out[:].unsqueeze(1).to_broadcast([P, QT, D]), ALU.add).then_inc(pool_xb, 1)
                    if prepares(s) and grp == 2:
                        wait(pool, act_part2, pre)
                        wait(pool, dma_scratch, pre + (-1), unit=16)
                        g.tensor_tensor(parts[:, :, 2, :], rest[:], parts[:, :, 1, :], ALU.subtract).then_inc(pool_part3, 1)
                if prepares(s + 1):
                    rstd_of(pre + 1)

            pool.wait_ge(pool_const, 8)
            rstd_of(Seq(0, 0))
            over_slots(pool.Fori, slot)

        @block.scalar
        def _(act):
            a = nc.scalar

            def take_exp(fin, grp):
                pr = probs[grp % 2]
                for j in range(3):
                    k = 3 * grp + j
                    wait(act, pe_scoreT, fin, per=ITEMS, k=k + 1)
                    if j == 0:
                        wait(act, pe_pv, fin, per=NG, k=grp - 1)
                    if j < 2:
                        o = pr[:, 0:3:2, 2 * j:2 * j + 2, :].rearrange("p b h c -> p h b c")
                        i = scoreT_ps[k % 2][:].rearrange("p (h b c) -> p h b c", h=2, b=2)
                    else:
                        o = pr[:, 1]
                        i = scoreT_ps[k % 2][:].rearrange("p (h q) -> p h q", h=HG)
                    a.activation(o, i, ACT.Exp, scale=SCALE).then_inc(act_exp, 1)

            def slot(t, s):
                pre, fin = t + 1, t + (-1)
                for grp in range(NG):
                    if finishes(s):
                        take_exp(fin, grp)
                    if grp == 0:
                        if prepares(s):
                            wait(act, pe_xnT, pre)
                            wait(act, pe_moe, pre + (-2), per=4)
                            a.copy(xnT[pre.par][:], m0[:, 0:S]).then_inc(act_xnT, 1)
                        if scores(s):
                            wait(act, dve_logits, t)
                            wait(act, pe_pv, t + (-2), per=NG)
                            if s <= 1:
                                act.wait_ge(dve_const, 1)
                            for q in range(QT):
                                v = vaug[t.par][:, q].rearrange("p h c -> p (h c)")
                                src = m1[:, q * VG:q * VG + D]
                                n3 = VGRP * HG
                                dst = bass.AP(tensor=v.tensor, offset=v.offset,
                                              ap=[list(v.ap[0]), [HG * VW + OW, VGRP], [VW, HG], [1, HD]])
                                a.copy(dst, src[:, 0:n3 * HD].rearrange("p (j c d) -> p j c d", j=VGRP, d=HD))
                                ins = a.copy(vaug[t.par][:, q, n3:H, 0:HD],
                                             src[:, n3 * HD:D].rearrange("p (c d) -> p c d", d=HD))
                            ins.then_inc(act_v, 1)
                    if grp == 1:
                        if prepares(s):
                            wait(act, pe_qk, pre)
                            wait(act, dma_scratch, pre + (-1), unit=16)
                            for c in range(2):
                                ins = a.activation(parts[:, c, 0, :], m2[:, c * S:(c + 1) * S], ACT.Identity,
                                                   bias=bqk_sb[:, c:c + 1])
                            ins.then_inc(act_part1, 1)
                    if grp == 2:
                        if prepares(s):
                            wait(act, dve_rest, pre)
                            a.copy(parts[:, :, 1, :], rest[:]).then_inc(act_part2, 1)
                        if scores(s):
                            wait(act, dve_gap, t)
                            a.activation(egap[:], gap[:], ACT.Exp).then_inc(act_gate, 1)
                if finishes(s):
                    wait(act, pe_pv, fin, per=NG)
                    wait(act, pe_o, fin + (-1))
                    a.copy(oT[:].rearrange("p r t -> p (r t)"), oT_ps[:]).then_inc(act_oT, 1)
                if scores(s):
                    wait(act, pe_mT, t)
                    wait(act, dma_max, t + (-1), unit=16)
                    a.copy(mT[:], m0[:].bitcast(BF16)[0:PARTS * H, 0:S]).then_inc(act_mT, 1)
                    wait(act, act_mT, t)
                    act.dma_start(qstack[t.par][MAX_ROW:ALL_ROWS], mT[:]).then_inc(dma_max, 16)
                if finishes(s):
                    wait(act, pe_oTn, fin)
                    wait(act, pe_y, fin + (-1))
                    a.copy(oTn[:], m0[:, 0:S]).then_inc(act_oTn, 1)

            act.wait_ge(ld_w, 16 * NW)
            over_slots(act.Fori, slot)

        @block.vector
        def _(dve):
            v = nc.vector

            def fill(b):
                v.memset(qstack[b][64:MAX_ROW], 0.0)
                v.memset(kstack[b][64:MAX_ROW], 0.0)
                v.memset(kstack[b][MAX_ROW:ALL_ROWS], 1.0)
                v.memset(vaug[b][:], 0.0)
            for b in range(2):
                fill(b)
            ones = []
            for b in range(2):
                for q in range(QT):
                    vv = vaug[b][:, q].rearrange("p h c -> p (h c)")
                    ones.append(bass.AP(tensor=vv.tensor, offset=vv.offset + HD,
                                        ap=[list(vv.ap[0]), [HG * VW + OW, VGRP], [VW, HG]]))
                    ones.append(vaug[b][:, q, VGRP * HG:H, HD])
            v.memset(bv_wide[:], 0.0).then_inc(dve_step, 1)
            dve.wait_ge(dve_step, 1)
            for o in ones:
                ins = v.memset(o, 1.0)
            ins.then_inc(dve_const, 1)
            dve.wait_ge(ld_w, 16 * NW)
            v.tensor_scalar(bv_wide[:], bv_wide[:], bv_sb[:], None, ALU.add).then_inc(dve_const, 1)

            def stats_of(n):
                wait_half(dve, dma_x[n.par], n)
                for q in range(QT):
                    ins = v.bn_stats(stats[:, q, :], x_sb[n.par][:, q, :])
                ins.then_inc(dve_step, 1)

            def aggregate():
                for q in range(QT):
                    ins = v.bn_aggr(mv[:, q, :], stats[:, q, :])
                ins.then_inc(dve_stats, 1)

            def slot(t, s):
                pre, fin = t + 1, t + (-1)
                k = [0]

                def step(ins):
                    ins.then_inc(dve_step, 1)
                    k[0] += 1

                def own():
                    dve.wait_ge(dve_step, base(t, s) + k[0])

                if prepares(s):
                    wait(dve, pool_rstd, pre)
                    wait(dve, pe_xnT, pre + (-1))
                    for q in range(QT):
                        ins = v.tensor_scalar(xn[:, q, :], x_sb[pre.par][:, q, :], mv[:, q, 0:1], rstd[:, q:q + 1],
                                              ALU.subtract, ALU.mult)
                    ins.then_inc(dve_xn, 1)
                for grp in range(NG):
                    if scores(s):
                        for j in range(3):
                            n = 3 * grp + j
                            wait(dve, pe_score, t, per=ITEMS, k=n + 1)
                            if n == 0:
                                wait(dve, dve_mparts, t + (-1))
                            if j == 0:
                                o, w = negmax[:, 0, HG * grp:HG * grp + HG], HG
                            else:
                                h0 = HG * grp + 2 * (j - 1)
                                o, w = negmax[:, 1, h0:h0 + 2], 2
                            v.tensor_reduce(o, score_ps[n % 2][:].rearrange("p (h k) -> p h k", h=w),
                                            axis=AX.X, op=ALU.max, negate=True).then_inc(dve_max, 1)
                    if grp == 0 and scores(s):
                        wait(dve, pe_vg, t)
                        vg = m1[:, 0:QT * VG].rearrange("p (q c) -> p q c", q=QT)
                        v.tensor_copy(logits[:], vg[:, :, D:VG]).then_inc(dve_logits, 1)
                    if grp == 1:
                        if scores(s):
                            wait(dve, dve_logits, t)
                            stand_alone(dve, dve_passed)
                            for q in range(QT):
                                ins = v.max(top[:, q, :], logits[:, q, :])
                            step(ins)
                        if prepares(s):
                            wait(dve, act_part1, pre)
                            wait(dve, pool_part3, pre + (-1))
                            for c in range(2):
                                ins = v.scalar_tensor_tensor(rest[:, c, :], m2[:, c * S:(c + 1) * S], bqk_sb[:, c:c + 1],
                                                             parts[:, c, 0, :], ALU.add, ALU.subtract)
                            ins.then_inc(dve_rest, 1)
                        if scores(s):
                            own()
                            v.tensor_tensor(gap[:], top[:, :, 1], top[:, :, 0], ALU.subtract).then_inc(dve_gap, 1)
                            for q in range(QT):
                                ins = v.max_index(topi[:, q, :], top[:, q, :], logits[:, q, :])
                            step(ins)
                            own()
                            step(v.tensor_copy(topf[:], topi[:, :, 0:2]))
                    if grp == 2 and scores(s):
                        wait(dve, act_gate, t)
                        step(v.tensor_scalar(egap1[:], egap[:], 1.0, None, ALU.add))
                        own()
                        step(v.reciprocal(gw[:, 0, :], egap1[:]))
                        own()
                        step(v.tensor_tensor(gw[:, 1, :], egap[:], gw[:, 0, :], ALU.mult))
                        own()
                        for q in range(QT):
                            for c in range(2):
                                ins = v.tensor_scalar(pick[:, c, q, :], expert_no[:], topf[:, q, c:c + 1], gw[:, c, q:q + 1],
                                                      ALU.is_equal, ALU.mult)
                        step(ins)
                        own()
                        v.tensor_tensor(weight[:], pick[:, 0], pick[:, 1], ALU.add).then_inc(dve_weight, 1)
                if scores(s):
                    wait(dve, dve_max, t, per=ITEMS)
                    wait(dve, pe_mT, t + (-1))
                    step(v.tensor_copy(mparts[:, :, 0, :], negmax[:]))
                    own()
                    step(v.tensor_tensor(mrest[:], negmax[:], mparts[:, :, 0, :], ALU.subtract))
                    own()
                    step(v.tensor_copy(mparts[:, :, 1, :], mrest[:]))
                    own()
                    v.tensor_tensor(mparts[:, :, 2, :], mrest[:], mparts[:, :, 1, :], ALU.subtract).then_inc(dve_mparts, 1)

                def experts(d):
                    q = d // 2
                    wait(dve, pe_moe, t, per=4, k=d + 1)
                    if d == 0:
                        wait(dve, dve_weight, t)
                        wait(dve, pool_xb, t)
                        wait(dve, dve_out, t + (-2))
                    for e in range(EH):
                        ex = EH * (d % 2) + e
                        before = xb[t.par][:, q, :] if ex == 0 else res[t.par][:, q, :]
                        if ex:
                            own()
                        ins = v.scalar_tensor_tensor(res[t.par][:, q, :], moe_ps[d % 2][:, e * D:(e + 1) * D],
                                                     weight[:, q, ex:ex + 1], before, ALU.mult, ALU.add)
                        if e < EH - 1:
                            step(ins)
                        else:
                            ins.then_inc(dve_moe, 1)
                            if d % 2 == 0:
                                wait(dve, dve_moe, t, per=4, k=d + 1)

                if scores(s):
                    experts(0)
                    experts(1)
                if finishes(s):
                    wait(dve, pe_o, fin)
                    wait(dve, pe_oTn, fin + (-1))
                    n3 = VGRP * HG
                    o4 = m0[:].rearrange("p (q r c w) -> p q r c w", q=QT, r=2, c=HG)
                    for q in range(QT):
                        den = o4[:, q, 0, :, 0:VGRP * OW].rearrange("p c (j w) -> p j c w", w=OW)
                        v.reciprocal(rden[:, q, 0:n3].rearrange("p (j c) -> p j c", c=HG), den[:, :, :, HD])
                        ins = v.reciprocal(rden[:, q, n3:H], o4[:, q, 1, :, HD])
                    step(ins)
                    own()
                    for q in range(QT):
                        num = o4[:, q, 0, :, 0:VGRP * OW].rearrange("p c (j w) -> p j c w", w=OW)
                        rd = rden[:, q, :].unsqueeze(2).to_broadcast([P, H, HD])
                        v.tensor_tensor(o_sb[:, q, 0:n3 * HD].rearrange("p (j c d) -> p j c d", j=VGRP, d=HD),
                                        num[:, :, :, 0:HD],
                                        rd[:, 0:n3, :].rearrange("p (j c) d -> p j c d", c=HG), ALU.mult)
                        ins = v.tensor_tensor(o_sb[:, q, n3 * HD:D].rearrange("p (c d) -> p c d", d=HD),
                                              o4[:, q, 1, :, 0:HD], rd[:, n3:H, :], ALU.mult)
                    ins.then_inc(dve_o, 1)
                if scores(s):
                    experts(2)
                    experts(3)
                if prepares(s + 1):
                    nxt = pre + 1
                    wait_half(dve, dma_x[nxt.par], nxt)
                    for q in range(QT):
                        ins = v.bn_stats(stats[:, q, :], x_sb[nxt.par][:, q, :])
                    step(ins)
                    own()
                    wait(dve, dve_xn, nxt + (-1))
                    stand_alone(dve, dve_passed)
                    for q in range(QT):
                        ins = v.bn_aggr(mv[:, q, :], stats[:, q, :])
                    ins.then_inc(dve_stats, 1)
                if finishes(s):
                    wait(dve, pe_y, fin)
                    wait(dve, dve_moe, fin, per=4)
                    if not (fin + (-2)).static or s >= 3:
                        wait_half(dve, dma_out[fin.par], fin + (-2))
                    v.tensor_tensor(out_sb[fin.par][:].rearrange("p q d -> p (q d)"), m0[:, 0:S],
                                    res[fin.par][:].rearrange("p q d -> p (q d)"), ALU.add).then_inc(dve_out, 1)
                counts[s] = k[0]

            dve.wait_ge(pe_bias, 1)
            dve.wait_ge(ld_bias, 16)
            v.tensor_tensor(bias_out[:], bias_out[:], m1[:, 0:D], ALU.add).then_inc(dve_bias, 1)
            wait_half(dve, dma_x[0], Seq(0, 0))
            for q in range(QT):
                ins = v.bn_stats(stats[:, q, :], x_sb[0][:, q, :])
            ins.then_inc(dve_step, 1)
            dve.wait_ge(dve_step, 2)
            for q in range(QT):
                ins = v.bn_aggr(mv[:, q, :], stats[:, q, :])
            ins.then_inc(dve_stats, 1)

            counts = {}

            def base(t, s):
                if s <= LOOP0 + 1:
                    before = 2 + sum(counts[x] for x in range(-1, s))
                    return before if t.static else before + t.i * (2 * FULL)
                return 2 + sum(counts[x] for x in range(-1, LOOP0)) + 2 * LOOPS * FULL \
                    + sum(counts[x] for x in range(LOOP0 + 2 * LOOPS, s))

            FULL = 2 + 1 + 3 + 1 + 3 + 4 * (EH - 1) + 1 + 1
            over_slots(dve.Fori, slot)
            assert counts[LOOP0] == counts[LOOP0 + 1] == FULL, (counts, FULL)

        @block.tensor
        def _(pe):
            tn = nc.tensor

            def score_item(t, grp, j):
                n = 3 * grp + j
                if n >= 2:
                    wait(pe, dve_max, t, per=ITEMS, k=n - 1)
                else:
                    wait(pe, dve_max, t + (-1), per=ITEMS, k=ITEMS + n - 1)
                if n == 0:
                    wait(pe, dma_stack, t, unit=16 * NSTACK)
                ps = score_ps[n % 2][:]
                qs, ks = qstack[t.par], kstack[t.par]
                if j == 0:
                    tn.matmul(ps.rearrange("p (h k) -> p h k", h=HG), ident_b[:],
                              mask_b[:].unsqueeze(1).to_broadcast([P, HG, P]), start=True, stop=False, skip_group_check=True)
                    for c in range(HG):
                        h = HG * grp + c
                        ins = tn.matmul(ps[:, c * P:(c + 1) * P], qs[0:MAX_ROW, h, 0:P], ks[0:MAX_ROW, h, 0:P],
                                        start=False, stop=c == HG - 1, skip_group_check=True)
                else:
                    tn.matmul(ps.rearrange("p (h b k) -> p h b k", h=2, b=2)[:, :, 1, :], ident_b[:],
                              mask_b[:].unsqueeze(1).to_broadcast([P, 2, P]), start=True, stop=False, skip_group_check=True)
                    for c in range(2):
                        h = HG * grp + 2 * (j - 1) + c
                        ins = tn.matmul(ps[:, c * S:(c + 1) * S], qs[0:MAX_ROW, h, P:S], ks[0:MAX_ROW, h, :],
                                        start=False, stop=c == 1, skip_group_check=True)
                ins.then_inc(pe_score, 1)

            def scoreT_item(f, grp, j):
                n = 3 * grp + j
                if n >= 2:
                    wait(pe, act_exp, f, per=ITEMS, k=n - 1)
                else:
                    wait(pe, act_exp, f + (-1), per=ITEMS, k=ITEMS + n - 1)
                if n == 0:
                    wait(pe, dma_max, f, unit=16)
                ps = scoreT_ps[n % 2][:]
                qs, ks = qstack[f.par], kstack[f.par]
                if j < 2:
                    for c in range(2):
                        h = HG * grp + 2 * j + c
                        ins = tn.matmul(ps[:, c * S:(c + 1) * S], ks[0:ALL_ROWS, h, 0:P], qs[0:ALL_ROWS, h, :],
                                        start=True, stop=True)
                else:
                    for c in range(HG):
                        h = HG * grp + c
                        ins = tn.matmul(ps[:, c * P:(c + 1) * P], ks[0:ALL_ROWS, h, P:S], qs[0:ALL_ROWS, h, P:S],
                                        start=True, stop=True)
                ins.then_inc(pe_scoreT, 1)

            def values(f, grp):
                wait(pe, pool_mask, f, per=NG, k=grp + 1)
                if grp == 0:
                    wait(pe, act_v, f)
                    wait(pe, act_oT, f + (-1))
                pr, va = probs[grp % 2], vaug[f.par]
                c0 = S if grp == NG - 1 else 0
                for q in range(QT):
                    for c in range(HG):
                        h = HG * grp + c
                        quad = slice(32 * c, 32 * c + 32)
                        o = oT_ps[quad, c0:c0 + S] if q == 0 else oT_ps[quad, c0 + P:c0 + S]
                        i = pr[:, 0:3:2, c, :] if q == 0 else pr[:, 1, c, :]
                        ins = tn.matmul(o, va[:, q, h, :], i, start=q == 0 and grp in (0, NG - 1),
                                        stop=q == 1 and grp in (NG - 2, NG - 1), skip_group_check=True)
                ins.then_inc(pe_pv, 1)

            def experts(t, s, d):
                q = d // 2
                if d >= 2:
                    wait(pe, dve_moe, t, per=4, k=d - 1)
                if d == 0:
                    wait(pe, act_v, t)
                if d == 1:
                    if prepares(s):
                        wait(pe, dve_rest, t + 1)
                    else:
                        wait(pe, dve_moe, t + (-1), per=4)
                tn.matmul(moe_ps[d % 2][:], xnT[t.par][:, q * P:(q + 1) * P],
                          we_sb[:, EH * (d % 2):EH * (d % 2 + 1), :].rearrange("p e m -> p (e m)"),
                          start=True, stop=True).then_inc(pe_moe, 1)

            def slot(t, s):
                pre, fin = t + 1, t + (-1)
                for grp in range(NG):
                    if scores(s):
                        for j in range(3):
                            score_item(t, grp, j)
                    if finishes(s):
                        for j in range(3):
                            scoreT_item(fin, grp, j)
                    if grp == 0:
                        if prepares(s):
                            wait(pe, dve_xn, pre)
                            wait(pe, act_mT, t + (-1))
                            wait(pe, dve_out, fin + (-1))
                            for q in range(QT):
                                ins = tn.transpose(m0[:, q * P:(q + 1) * P], xn[:, q, :], ident[:])
                            ins.then_inc(pe_xnT, 1)
                        if scores(s):
                            wait(pe, act_xnT, t)
                            wait(pe, dve_moe, t + (-1), per=4)
                            if s == 0:
                                pe.wait_ge(dve_bias, 1)
                            for q in range(QT):
                                ins = tn.matmul(m1[:, q * VG:(q + 1) * VG], xnT[t.par][:, q * P:(q + 1) * P], wvg_sb[:],
                                                start=True, stop=True)
                            ins.then_inc(pe_vg, 1)
                    if grp == 1 and prepares(s):
                        wait(pe, act_xnT, pre)
                        wait(pe, dve_moe, t + (-1), per=4)
                        for c in range(2):
                            ins = tn.matmul(m2[:, c * S:(c + 1) * S], wqk_sb[:, c, :], xnT[pre.par][:], start=True, stop=True)
                        ins.then_inc(pe_qk, 1)
                    if finishes(s) and grp >= 1:
                        values(fin, grp - 1)
                if finishes(s):
                    values(fin, NG - 1)
                if scores(s):
                    experts(t, s, 0)
                    wait(pe, dve_mparts, t)
                    if prepares(s):
                        wait(pe, act_xnT, pre)
                    else:
                        wait(pe, dve_out, fin + (-1))
                    stand_alone(pe, pe_passed)
                    mTp = m0[:].bitcast(BF16)
                    for q in range(QT):
                        ins = tn.transpose(mTp[0:PARTS * H, q * P:(q + 1) * P],
                                           mparts[:, q].rearrange("p a h -> p (a h)"), ident_b[:])
                    ins.then_inc(pe_mT, 1)
                    experts(t, s, 1)
                if finishes(s):
                    wait(pe, act_oT, fin)
                    wait(pe, act_mT, t if scores(s) else fin)
                    if not scores(s):
                        wait(pe, dve_out, fin + (-1))
                    for q in range(QT):
                        for r in range(2):
                            c = (q * 2 + r) * P
                            ins = tn.transpose(m0[:, c:c + P], oT[:, r, q * P:(q + 1) * P], ident[:])
                    ins.then_inc(pe_o, 1)
                if scores(s):
                    experts(t, s, 2)
                if finishes(s):
                    wait(pe, dve_o, fin)
                    for q in range(QT):
                        ins = tn.transpose(m0[:, q * P:(q + 1) * P], o_sb[:, q, :], ident[:])
                    ins.then_inc(pe_oTn, 1)
                if scores(s):
                    experts(t, s, 3)
                if finishes(s):
                    wait(pe, act_oTn, fin)
                    for q in range(QT):
                        ins = tn.matmul(m0[:, q * P:(q + 1) * P], oTn[:, q * P:(q + 1) * P], wo_sb[:], start=True, stop=True)
                    ins.then_inc(pe_y, 1)

            pe.wait_ge(pool_const, 8)
            pe.wait_ge(ld_w, 16 * NW)
            pe.wait_ge(dve_const, 2)
            tn.matmul(m1[:, 0:D], bv_wide[:], wo_sb[:], start=True, stop=True).then_inc(pe_bias, 1)
            over_slots(pe.Fori, slot)


def kernel(L0_attn_x, L0_attn_Wq, L0_attn_bq, L0_attn_Wk, L0_attn_bk, L0_attn_Wv, L0_attn_bv,
           L0_attn_Wo, L0_attn_bo, L0_ffn_gate_w, L0_ffn_We):
    import numpy as np
    import concourse.bacc as bacc
    from concourse.bass_utils import run_bass_kernel_spmd

    def by_feature(w):
        w = np.asarray(w)
        return np.swapaxes(w.reshape((H, HD) + w.shape[1:]), 0, 1).reshape(w.shape)

    host = {
        "x": np.asarray(L0_attn_x).reshape(NSEQ * S, D),
        "wq": by_feature(L0_attn_Wq).T, "wk": by_feature(L0_attn_Wk).T,
        "bq": by_feature(L0_attn_bq), "bk": by_feature(L0_attn_bk),
        "wv": np.asarray(L0_attn_Wv).T, "bv": np.asarray(L0_attn_bv),
        "wo": np.asarray(L0_attn_Wo).T, "bo": np.asarray(L0_attn_bo),
        "gate": np.asarray(L0_ffn_gate_w).T, "we": np.asarray(L0_ffn_We),
    }
    nc = bacc.Bacc("TRN2", target_bir_lowering=False, num_devices=1)
    arrays, args = {}, {}
    for name, a in host.items():
        arrays[f"in_{name}"] = np.ascontiguousarray(a)
        args[name] = nc.dram_tensor(f"in_{name}", a.shape, FP32, kind="ExternalInput").ap()
    out = nc.dram_tensor("out", (NSEQ * S, D), FP32, kind="ExternalOutput").ap()
    bass_block(nc, out=out, **args)
    r = run_bass_kernel_spmd(nc, [arrays], core_ids=[0])
    return r.results[0]["out"].reshape(NSEQ, S, D)
```

```python
from contextlib import ExitStack

import concourse.bass as bass
from concourse import mybir

FP32 = mybir.dt.float32
BF16 = mybir.dt.bfloat16
U32 = mybir.dt.uint32
ALU = mybir.AluOpType
ACT = mybir.ActivationFunctionType
AX = mybir.AxisListType

NSEQ, S, D = 32, 256, 128
H, HD = 16, 8
E = 8
P = 128
QT = S // P
NB = 3
PARTS = 3
PART_ROWS = PARTS * HD
PROD_ROWS = PARTS * PART_ROWS
MAX_ROW = 96
ALL_ROWS = MAX_ROW + PARTS
HG = 4
NG = H // HG
ITEMS = 3 * NG
LAG = 4
VW = 32
VGRP = 3
OW = HD + 1
VG = D + E
EH = 4
MASKS = 2 * NG
SCALE = float(HD) ** -0.5
EPS = 1e-5
MASKED = -3.0e38
TOP, INDEX, FLOAT, HIT, TOTAL, FIRST, SECOND, SHARE, WEIGHT = range(1, 10)
SUM_Q0, SUM_Q1, PAIRS, FOURS, RESULT = range(1, 6)


def stand_alone(eng, passed):
    eng.sem_inc(passed, 1)


class Seq:

    def __init__(self, i, c):
        self.i, self.c = i, c

    def __add__(self, k):
        return Seq(self.i, self.c + k)

    @property
    def n(self):
        return self.i * NB + self.c

    @property
    def buf(self):
        return self.c % NB

    @property
    def turn(self):
        return self.i + self.c // NB

    @property
    def none(self):
        return isinstance(self.i, int) and self.n < 0


def upto(seq, per=1, k=None, unit=1):
    return 0 if seq.none else (seq.n * per + (per if k is None else k)) * unit


def bass_block(nc, x, wq, wk, bq, bk, wv, bv, wo, bo, gate, we, out):
    ctx = ExitStack()
    with ctx:
        def sb(name, shape, dt=FP32):
            return ctx.enter_context(nc.sbuf_tensor(name, shape, dt))

        def sbs(name, shape, dt=FP32, n=NB):
            return [sb(f"{name}{b}", shape, dt) for b in range(n)]

        def pb(name):
            return ctx.enter_context(nc.psum_tensor(name, [P, 512], FP32))

        def sem(name):
            return ctx.enter_context(nc.semaphore(name))

        def sems(*names):
            return [sem(n) for n in names]

        wqk_sb = sb("wqk_sb", [P, 2, D])
        bqk_sb = sb("bqk_sb", [P, 2])
        wvg_sb = sb("wvg_sb", [P, VG])
        wo_sb = sb("wo_sb", [P, D])
        we_sb = sb("we_sb", [P, E, D])
        bv_sb = sb("bv_sb", [P, 1])
        bv_wide = sb("bv_wide", [P, P])
        bias_out = sb("bias_out", [P, D])
        ident = sb("ident", [P, P])
        ident_b = sb("ident_b", [P, P], BF16)
        mask_b = sb("mask_b", [P, P], BF16)
        expert_no = sb("expert_no", [P, E])
        minus_half = sb("minus_half", [P, QT])
        x_sb = sbs("x_sb", [P, QT, D])
        xb = sbs("xb", [P, QT, D])
        xnT = sbs("xnT", [P, S])
        qstack = sbs("qstack", [P, H, S], BF16)
        kstack = sbs("kstack", [P, H, S], BF16)
        vaug = sbs("vaug", [P, QT, H, VW])
        negmax = sbs("negmax", [P, QT, H])
        weight = sbs("weight", [P, QT, E])
        probs = sbs("probs", [P, 3, HG, P], n=2)
        stats = sb("stats", [P, QT, 6])
        mv = sb("mv", [P, QT, 2])
        var_eps = sb("var_eps", [P, QT])
        rstd = sb("rstd", [P, QT])
        xn = sb("xn", [P, QT, D])
        parts = sb("parts", [P, 2, PARTS, S], BF16)
        rest = sb("rest", [P, 2, S])
        mrest = sb("mrest", [P, QT, H])
        mparts = sb("mparts", [P, QT, PARTS, H], BF16)
        mT = sb("mT", [PARTS * H, S], BF16)
        logits = sb("logits", [P, QT, E])
        top = sb("top", [P, QT, 8])
        topi = sb("topi", [P, QT, 8], U32)
        topf = sb("topf", [P, QT, 2])
        gap = sb("gap", [P, QT])
        egap = sb("egap", [P, QT])
        egap1 = sb("egap1", [P, QT])
        gw = sb("gw", [P, QT, 2])
        hit = sb("hit", [P, QT, 2, E])
        share = sb("share", [P, QT, 2, E])
        lower = sb("lower", [P, EH, QT, D])
        upper = sb("upper", [P, EH, QT, D])
        fours = sb("fours", [P, EH, QT, D])
        pairs = sb("pairs", [P, 2, QT, D])
        mixed = sb("mixed", [P, QT, D])
        out_sb = sb("out_sb", [P, QT, D])
        res = sb("res", [P, QT, D])
        oT = sb("oT", [P, 2, S])
        rden = sb("rden", [P, QT, H])
        o_sb = sb("o_sb", [P, QT, D])
        oTn = sb("oTn", [P, S])

        score_ps = [pb(f"score_ps{b}") for b in range(2)]
        scoreT_ps = [pb(f"scoreT_ps{b}") for b in range(2)]
        oT_ps = pb("oT_ps")
        m0, m1, m2 = pb("m0"), pb("m1"), pb("m2")
        moe_ps = [m1, m2]

        scratch = [nc.dram_tensor(f"scratch{b}", [2, PARTS, P, S], BF16, kind="Internal").ap() for b in range(NB)]

        ld_qk, ld_w, ld_we, ld_bias, pool_const, dve_const, pe_bias, dve_bias = sems(
            "ld_qk", "ld_w", "ld_we", "ld_bias", "pool_const", "dve_const", "pe_bias", "dve_bias")
        pool_fill, dve_fill, dve_zero = sems("pool_fill", "dve_fill", "dve_zero")
        dma_x = sems(*(f"dma_x{b}" for b in range(NB)))
        dma_scratch = sems("dma_scratch_q", "dma_scratch_k")
        dma_stack, dma_max, dma_out = sems("dma_stack", "dma_max", "dma_out")
        dve_stats, dve_mv, pool_eps, pool_rstd, dve_xn = sems("dve_stats", "dve_mv", "pool_eps", "pool_rstd", "dve_xn")
        pe_xnT, act_xnT, pool_xb = sems("pe_xnT", "act_xnT", "pool_xb")
        pe_qk, act_part1, dve_rest, act_part2, pool_part3 = sems("pe_qk", "act_part1", "dve_rest", "act_part2", "pool_part3")
        pe_score, dve_max, dve_mpart, pe_mT, act_mT = sems("pe_score", "dve_max", "dve_mpart", "pe_mT", "act_mT")
        pe_vg, act_v, dve_gap, act_gate, dve_gate = sems(
            "pe_vg", "act_v", "dve_gap", "act_gate", "dve_gate")
        pe_scoreT, act_exp, pool_mask, pe_pv, act_oT = sems("pe_scoreT", "act_exp", "pool_mask", "pe_pv", "act_oT")
        pe_moe, dve_lower, act_upper, pool_sum = sems("pe_moe", "dve_lower", "act_upper", "pool_sum")
        pe_o, dve_den, dve_o, pe_oTn, act_oTn, pe_y, dve_out = sems(
            "pe_o", "dve_den", "dve_o", "pe_oTn", "act_oTn", "pe_y", "dve_out")
        pool_passed, dve_passed, pe_passed, sp_passed = sems("pool_passed", "dve_passed", "pe_passed", "sp_passed")

        NSTACK = 4
        NQK, NW = 4, 4
        LOOP0 = 3
        LOOPS = (NSEQ - 2 - LOOP0) // NB

        x_t = x.rearrange("(s q p) d -> s p q d", q=QT, p=P)
        out_t = out.rearrange("(s q p) d -> s p q d", q=QT, p=P)

        def over_slots(eng_fori, slot, between=None):
            for s in range(-2, LOOP0):
                slot(Seq(0, s), s)
                if between:
                    between(s)
            with eng_fori(0, LOOPS) as i:
                for u in range(NB):
                    slot(Seq(i, LOOP0 + u), LOOP0 + u)
            for s in range(LOOP0 + NB * LOOPS, NSEQ + 2):
                slot(Seq(0, s), s)

        def has(s, k):
            return 0 <= s + k < NSEQ

        def behind(t, s, n):
            k = -1 if n >= LAG else -2
            return (t + k, (n - LAG) % ITEMS) if has(s, k) else (None, None)

        block = ctx.enter_context(nc.Block())

        @block.sync
        def _(sp):
            sp.dma_start(x_sb[0][:], x_t[0]).then_inc(dma_x[0], 16)
            sp.dma_start(wqk_sb[:, 0, :], wq).then_inc(ld_qk, 16)
            sp.dma_start(wqk_sb[:, 1, :], wk).then_inc(ld_qk, 16)
            sp.dma_start(bqk_sb[:, 0:1], bq.unsqueeze(1)).then_inc(ld_qk, 16)
            sp.dma_start(bqk_sb[:, 1:2], bk.unsqueeze(1)).then_inc(ld_qk, 16)
            sp.dma_start(wvg_sb[:, 0:D], wv).then_inc(ld_w, 16)
            sp.dma_start(wvg_sb[:, D:VG], gate).then_inc(ld_w, 16)
            sp.dma_start(wo_sb[:], wo).then_inc(ld_w, 16)
            sp.dma_start(bv_sb[:], bv.unsqueeze(1)).then_inc(ld_w, 16)
            sp.dma_start(bias_out[:], bo.unsqueeze(0).to_broadcast([P, D])).then_inc(ld_bias, 16)

            def store(fin):
                sp.wait_ge(dve_out, upto(fin))
                sp.dma_start(out_t[fin.n], out_sb[:]).then_inc(dma_out, 16)

            def slot(t, s):
                if has(s, -3):
                    store(t + (-3))
                if has(s, 2) and s > -2:
                    nxt = t + 2
                    sp.wait_ge(dve_xn, upto(nxt + (-NB)))
                    sp.wait_ge(pool_xb, upto(nxt + (-NB)))
                    sp.dma_start(x_sb[nxt.buf][:], x_t[nxt.n]).then_inc(dma_x[nxt.buf], 16)
                if s == -1:
                    sp.dma_start(we_sb[:], we.rearrange("e d m -> d e m")).then_inc(ld_we, 16)
                if has(s, 1):
                    pre, last = t + 1, t + (1 - NB)
                    scr = scratch[pre.buf]
                    sp.wait_ge(act_part1, upto(pre))
                    stand_alone(sp, sp_passed)
                    for c in range(2):
                        sp.wait_ge(act_part2, upto(pre, per=2, k=c + 1))
                        sp.wait_ge(pool_part3, upto(pre, per=2, k=c + 1))
                        sp.dma_start(scr[c].rearrange("a r t -> r a t"), parts[:, c]).then_inc(dma_scratch[c], 16)
                    sp.wait_ge(pe_scoreT, upto(last, per=ITEMS))
                    sp.wait_ge(pe_score, upto(last, per=ITEMS))
                    stand_alone(sp, sp_passed)
                    if s < 2:
                        sp.wait_ge(*((dve_fill, 1), (pool_fill, 2), (pool_fill, 4))[s + 1])
                    rows = scr.rearrange("c a (d h) t -> c (a d) (h t)", h=H)
                    qs, ks = (st[pre.buf][:].rearrange("p h t -> p (h t)") for st in (qstack, kstack))
                    sp.wait_ge(dma_scratch[0], upto(pre, unit=16))
                    for a in range(PARTS):
                        part = rows[0, a * HD:(a + 1) * HD].unsqueeze(0).to_broadcast([PARTS, HD, H * S])
                        sp.dma_start(qs[a * PART_ROWS:(a + 1) * PART_ROWS], part).then_inc(dma_stack, 16)
                    sp.wait_ge(dma_scratch[1], upto(pre, unit=16))
                    sp.dma_start(ks[0:PROD_ROWS],
                                 rows[1].unsqueeze(0).to_broadcast([PARTS, PART_ROWS, H * S])).then_inc(dma_stack, 16)

            over_slots(sp.Fori, slot)
            store(Seq(0, NSEQ - 1))
            sp.wait_ge(dma_out, upto(Seq(0, NSEQ - 1), unit=16))

        @block.gpsimd
        def _(pool):
            g = nc.gpsimd
            g.memset(minus_half[:], -0.5).then_inc(pool_const, 1)
            g.memset(ident[:], 0.0).then_inc(pool_const, 1)
            g.memset(ident_b[:], 0.0).then_inc(pool_const, 1)
            g.memset(mask_b[:], 0.0).then_inc(pool_const, 1)
            g.iota(expert_no[:], pattern=[[1, E]], base=0, channel_multiplier=0,
                   allow_small_or_imprecise_dtypes=True).then_inc(pool_const, 1)
            pool.wait_ge(pool_const, 5)
            for m in (ident, ident_b):
                g.affine_select(out=m[:], in_=m[:], compare_op=ALU.not_equal, fill=1.0, base=0,
                                pattern=[[-1, P]], channel_multiplier=1).then_inc(pool_const, 1)
            g.affine_select(out=mask_b[:], in_=mask_b[:], compare_op=ALU.is_ge, fill=MASKED, base=0,
                            pattern=[[-1, P]], channel_multiplier=1).then_inc(pool_const, 1)

            def mask(f, grp, block_no):
                k = 3 * grp + 2 + block_no
                pool.wait_ge(act_exp, upto(f, per=ITEMS, k=k))
                stand_alone(pool, pool_passed)
                pr = probs[grp % 2][:, block_no]
                g.affine_select(out=pr, in_=pr, compare_op=ALU.is_ge, fill=0.0, base=0,
                                pattern=[[0, HG], [1, P]], channel_multiplier=-1).then_inc(pool_mask, 1)

            def part3(pre, c):
                pool.wait_ge(act_part2, upto(pre, per=2, k=c + 1))
                pool.wait_ge(dma_scratch[c], upto(pre + (-1), unit=16))
                g.tensor_tensor(parts[:, c, 2, :], rest[:, c, :], parts[:, c, 1, :], ALU.subtract).then_inc(pool_part3, 1)

            def sum_tile(m, q):
                pool.wait_ge(dve_lower, upto(m, per=2, k=q + 1))
                pool.wait_ge(act_upper, upto(m, per=2, k=q + 1))
                g.tensor_tensor(fours[:, :, q, :], lower[:, :, q, :], upper[:, :, q, :], ALU.add).then_inc(pool_sum, 1)

            def slot(t, s):
                for n in range(ITEMS):
                    f, k = behind(t, s, n)
                    if f and k % 3:
                        mask(f, k // 3, k % 3 - 1)
                    if n == 1 and has(s, -2):
                        m = t + (-2)
                        sum_tile(m, 1)
                    if n == 3 and has(s, -2):
                        m = t + (-2)
                        pool.wait_ge(pool_sum, upto(m, per=RESULT, k=SUM_Q1))
                        g.tensor_tensor(pairs[:], fours[:, 0:2], fours[:, 2:4], ALU.add).then_inc(pool_sum, 1)
                    if n in (4, 5) and has(s, 1):
                        part3(t + 1, n - 4)
                    if n == 6 and has(s, -2):
                        m = t + (-2)
                        pool.wait_ge(pool_sum, upto(m, per=RESULT, k=PAIRS))
                        g.tensor_tensor(mixed[:], pairs[:, 0], pairs[:, 1], ALU.add).then_inc(pool_sum, 1)
                    if n == 7 and has(s, -2):
                        m = t + (-2)
                        pool.wait_ge(pool_sum, upto(m, per=RESULT, k=FOURS))
                        pool.wait_ge(pool_xb, upto(m))
                        pool.wait_ge(dve_out, upto(m + (-1)))
                        g.tensor_tensor(res[:], mixed[:], xb[m.buf][:], ALU.add).then_inc(pool_sum, 1)
                    if n == 9 and has(s, 0):
                        pool.wait_ge(dma_x[t.buf], 16 * (t.turn + 1))
                        if s == 0:
                            pool.wait_ge(dve_bias, 1)
                        g.tensor_tensor(xb[t.buf][:], x_sb[t.buf][:],
                                        bias_out[:].unsqueeze(1).to_broadcast([P, QT, D]), ALU.add).then_inc(pool_xb, 1)
                    if n == 8 and has(s, 2):
                        nxt = t + 2
                        pool.wait_ge(dve_mv, upto(nxt))
                        pool.wait_ge(dve_xn, upto(nxt + (-1)))
                        stand_alone(pool, pool_passed)
                        g.tensor_scalar(var_eps[:], mv[:, :, 1], 1.0, EPS, ALU.mult, ALU.add).then_inc(pool_eps, 1)
                        pool.wait_ge(pool_eps, upto(nxt))
                        g.tensor_tensor(rstd[:], var_eps[:], minus_half[:], ALU.pow).then_inc(pool_rstd, 1)
                    if n == 10 and has(s, -1):
                        sum_tile(t + (-1), 0)

            def between(s):
                if -1 <= s < NB - 2:
                    g.memset(qstack[s + 2][:], 0.0).then_inc(pool_fill, 1)
                    g.memset(kstack[s + 2][:], 1.0).then_inc(pool_fill, 1)

            over_slots(pool.Fori, slot, between)

        @block.scalar
        def _(act):
            a = nc.scalar

            def take_exp(f, k):
                grp, j = k // 3, k % 3
                pr = probs[grp % 2]
                act.wait_ge(pe_scoreT, upto(f, per=ITEMS, k=k + 1))
                if j == 0:
                    if grp >= 2:
                        act.wait_ge(pe_pv, upto(f, per=NG, k=grp - 1))
                    else:
                        act.wait_ge(pe_pv, upto(f + (-1), per=NG, k=NG + grp - 1))
                if j < 2:
                    o = pr[:, 0:3:2, 2 * j:2 * j + 2, :].rearrange("p b h c -> p h b c")
                    i = scoreT_ps[k % 2][:].rearrange("p (h b c) -> p h b c", h=2, b=2)
                else:
                    o = pr[:, 1]
                    i = scoreT_ps[k % 2][:].rearrange("p (h q) -> p h q", h=HG)
                a.activation(o, i, ACT.Exp, scale=SCALE).then_inc(act_exp, 1)

            def take_values(t, s):
                act.wait_ge(pe_vg, upto(t))
                act.wait_ge(dve_gate, upto(t + (-1), per=WEIGHT, k=INDEX))
                a.copy(logits[:], m1[:, 0:QT * VG].rearrange("p (q c) -> p q c", q=QT)[:, :, D:VG])
                act.wait_ge(pe_pv, upto(t + (-NB), per=NG))
                if s < NB:
                    act.wait_ge(dve_fill, 2 + s)
                for q in range(QT):
                    v = vaug[t.buf][:, q].rearrange("p h c -> p (h c)")
                    src = m1[:, q * VG:q * VG + D]
                    n3 = VGRP * HG
                    dst = bass.AP(tensor=v.tensor, offset=v.offset,
                                  ap=[list(v.ap[0]), [HG * VW + OW, VGRP], [VW, HG], [1, HD]])
                    a.copy(dst, src[:, 0:n3 * HD].rearrange("p (j c d) -> p j c d", j=VGRP, d=HD))
                    ins = a.copy(vaug[t.buf][:, q, n3:H, 0:HD], src[:, n3 * HD:D].rearrange("p (c d) -> p c d", d=HD))
                ins.then_inc(act_v, 1)

            def part1(pre):
                act.wait_ge(pe_qk, upto(pre))
                for c in range(2):
                    act.wait_ge(dma_scratch[c], upto(pre + (-1), unit=16))
                    ins = a.activation(parts[:, c, 0, :], m2[:, c * S:(c + 1) * S], ACT.Identity, bias=bqk_sb[:, c:c + 1])
                ins.then_inc(act_part1, 1)

            def part2(pre, c):
                act.wait_ge(dve_rest, upto(pre, per=2, k=c + 1))
                a.copy(parts[:, c, 1, :], rest[:, c, :]).then_inc(act_part2, 1)

            def upper_experts(m, q):
                act.wait_ge(pe_moe, upto(m, per=4, k=2 * q + 2))
                act.wait_ge(dve_gate, upto(m, per=WEIGHT))
                act.wait_ge(pool_sum, upto(m + (-1), per=RESULT, k=q + 1))
                for e in range(EH):
                    ins = a.activation(upper[:, e, q, :], m2[:, e * D:(e + 1) * D], ACT.Copy,
                                       scale=weight[m.buf][:, q, EH + e:EH + e + 1])
                ins.then_inc(act_upper, 1)

            def slot(t, s):
                for n in range(ITEMS):
                    if n == 2 and has(s, 1):
                        part1(t + 1)
                    if n == 0 and has(s, 0):
                        take_values(t, s)
                    if n == 0 and has(s, 1):
                        act.wait_ge(pe_xnT, upto(t + 1))
                        act.wait_ge(pe_moe, upto(t + (1 - NB), per=4))
                        a.copy(xnT[(t + 1).buf][:], m2[:, 0:S]).then_inc(act_xnT, 1)
                    if n == 11 and has(s, -1):
                        upper_experts(t + (-1), 1)
                    f, k = behind(t, s, n)
                    if f:
                        take_exp(f, k)
                    if n == 1 and has(s, -1):
                        m = t + (-1)
                        act.wait_ge(pe_mT, upto(m))
                        act.wait_ge(dma_max, upto(m + (-1), unit=16))
                        a.copy(mT[:], m0[:].bitcast(BF16)[0:PARTS * H, 0:S]).then_inc(act_mT, 1)
                        act.wait_ge(act_mT, upto(m))
                        act.dma_start(qstack[m.buf][MAX_ROW:ALL_ROWS], mT[:]).then_inc(dma_max, 16)
                    if n == 5 and has(s, -2):
                        fin = t + (-2)
                        act.wait_ge(pe_pv, upto(fin, per=NG))
                        act.wait_ge(pe_o, upto(fin + (-1)))
                        a.copy(oT[:].rearrange("p r t -> p (r t)"), oT_ps[:]).then_inc(act_oT, 1)
                    if n in (4, 5) and has(s, 1):
                        part2(t + 1, n - 4)
                    if n == 5 and has(s, 0):
                        act.wait_ge(dve_gap, upto(t))
                        a.activation(egap[:], gap[:], ACT.Exp).then_inc(act_gate, 1)
                    if n == 10 and has(s, -2):
                        fin = t + (-2)
                        act.wait_ge(pe_oTn, upto(fin))
                        act.wait_ge(pe_y, upto(fin + (-1)))
                        a.copy(oTn[:], m0[:, 0:S]).then_inc(act_oTn, 1)
                    if n == 6 and has(s, -1):
                        upper_experts(t + (-1), 0)

            act.wait_ge(ld_qk, 16 * NQK)
            over_slots(act.Fori, slot)

        @block.vector
        def _(dve):
            v = nc.vector
            n3 = VGRP * HG

            def take_max(t, n):
                dve.wait_ge(pe_score, upto(t, per=ITEMS, k=n + 1))
                grp, j = n // 3, n % 3
                if j == 0:
                    o, w = negmax[t.buf][:, 0, HG * grp:HG * grp + HG], HG
                else:
                    h0 = HG * grp + 2 * (j - 1)
                    o, w = negmax[t.buf][:, 1, h0:h0 + 2], 2
                v.tensor_reduce(o, score_ps[n % 2][:].rearrange("p (h k) -> p h k", h=w),
                                axis=AX.X, op=ALU.max, negate=True).then_inc(dve_max, 1)

            def gates(t, k):
                if k == TOP:
                    dve.wait_ge(act_v, upto(t))
                    stand_alone(dve, dve_passed)
                    for q in range(QT):
                        ins = v.max(top[:, q, :], logits[:, q, :])
                if k == INDEX:
                    dve.wait_ge(dve_gate, upto(t, per=WEIGHT, k=TOP))
                    v.tensor_tensor(gap[:], top[:, :, 1], top[:, :, 0], ALU.subtract).then_inc(dve_gap, 1)
                    for q in range(QT):
                        ins = v.max_index(topi[:, q, :], top[:, q, :], logits[:, q, :])
                if k == FLOAT:
                    dve.wait_ge(dve_gate, upto(t, per=WEIGHT, k=INDEX))
                    ins = v.tensor_copy(topf[:], topi[:, :, 0:2])
                if k == HIT:
                    dve.wait_ge(dve_gate, upto(t, per=WEIGHT, k=FLOAT))
                    ins = v.tensor_tensor(hit[:], expert_no[:].unsqueeze(1).unsqueeze(1).to_broadcast([P, QT, 2, E]),
                                          topf[:].unsqueeze(3).to_broadcast([P, QT, 2, E]), ALU.is_equal)
                if k == TOTAL:
                    dve.wait_ge(act_gate, upto(t))
                    ins = v.tensor_scalar(egap1[:], egap[:], 1.0, None, ALU.add)
                if k == FIRST:
                    dve.wait_ge(dve_gate, upto(t, per=WEIGHT, k=TOTAL))
                    ins = v.reciprocal(gw[:, :, 0], egap1[:])
                if k == SECOND:
                    dve.wait_ge(dve_gate, upto(t, per=WEIGHT, k=FIRST))
                    ins = v.tensor_tensor(gw[:, :, 1], egap[:], gw[:, :, 0], ALU.mult)
                if k == SHARE:
                    dve.wait_ge(dve_gate, upto(t, per=WEIGHT, k=SECOND))
                    ins = v.tensor_tensor(share[:], hit[:], gw[:].unsqueeze(3).to_broadcast([P, QT, 2, E]), ALU.mult)
                if k == WEIGHT:
                    dve.wait_ge(dve_gate, upto(t, per=WEIGHT, k=SHARE))
                    dve.wait_ge(pe_moe, upto(t + (-NB), per=4))
                    ins = v.tensor_tensor(weight[t.buf][:], share[:, :, 0], share[:, :, 1], ALU.add)
                ins.then_inc(dve_gate, 1)

            def lower_experts(m, q):
                dve.wait_ge(pe_moe, upto(m, per=4, k=2 * q + 1))
                dve.wait_ge(dve_gate, upto(m, per=WEIGHT))
                dve.wait_ge(pool_sum, upto(m + (-1), per=RESULT, k=q + 1))
                v.tensor_tensor(lower[:, :, q, :], m1[:].rearrange("p (e m) -> p e m", e=EH),
                                weight[m.buf][:, q, 0:EH].unsqueeze(2).to_broadcast([P, EH, D]),
                                ALU.mult).then_inc(dve_lower, 1)

            def max_parts(t, k):
                if k == 0:
                    dve.wait_ge(dve_max, upto(t, per=ITEMS))
                    dve.wait_ge(pe_mT, upto(t + (-1)))
                    ins = v.tensor_copy(mparts[:, :, 0, :], negmax[t.buf][:])
                else:
                    dve.wait_ge(dve_mpart, upto(t, per=4, k=k))
                if k == 1:
                    ins = v.tensor_tensor(mrest[:], negmax[t.buf][:], mparts[:, :, 0, :], ALU.subtract)
                if k == 2:
                    ins = v.tensor_copy(mparts[:, :, 1, :], mrest[:])
                if k == 3:
                    ins = v.tensor_tensor(mparts[:, :, 2, :], mrest[:], mparts[:, :, 1, :], ALU.subtract)
                ins.then_inc(dve_mpart, 1)

            def outputs(q):
                o4 = m0[:].rearrange("p (q r c w) -> p q r c w", q=QT, r=2, c=HG)
                return o4[:, q, 0, :, 0:VGRP * OW].rearrange("p c (j w) -> p j c w", w=OW), o4[:, q, 1, :, 0:OW]

            def slot(t, s):
                fin = t + (-2)
                for n in range(ITEMS):
                    if has(s, 0):
                        take_max(t, n)
                    if n == 1 and has(s, 0):
                        gates(t, TOP)
                    if n in (3, 4) and has(s, 1):
                        pre, c = t + 1, n - 3
                        dve.wait_ge(act_part1, upto(pre))
                        dve.wait_ge(pool_part3, upto(pre + (-1), per=2))
                        v.scalar_tensor_tensor(rest[:, c, :], m2[:, c * S:(c + 1) * S], bqk_sb[:, c:c + 1],
                                               parts[:, c, 0, :], ALU.add, ALU.subtract).then_inc(dve_rest, 1)
                    if n == 4 and has(s, 0):
                        gates(t, INDEX)
                    if n == 5 and has(s, 0):
                        gates(t, FLOAT)
                    if n == 5 and has(s, -1):
                        lower_experts(t + (-1), 0)
                    if n == 6 and has(s, 0):
                        gates(t, HIT)
                        gates(t, TOTAL)
                    if n == 7 and has(s, 0):
                        gates(t, FIRST)
                    if n == 7 and has(s, 2):
                        nxt = t + 2
                        dve.wait_ge(dma_x[nxt.buf], 16 * (nxt.turn + 1))
                        for q in range(QT):
                            ins = v.bn_stats(stats[:, q, :], x_sb[nxt.buf][:, q, :])
                        ins.then_inc(dve_stats, 1)
                    if n == 8 and has(s, 0):
                        gates(t, SECOND)
                    if n == 8 and has(s, 2):
                        nxt = t + 2
                        dve.wait_ge(dve_stats, upto(nxt))
                        dve.wait_ge(pool_eps, upto(nxt + (-1)))
                        stand_alone(dve, dve_passed)
                        for q in range(QT):
                            ins = v.bn_aggr(mv[:, q, :], stats[:, q, :])
                        ins.then_inc(dve_mv, 1)
                    if n == 8 and has(s, -2):
                        dve.wait_ge(pe_o, upto(fin))
                        for q in range(QT):
                            first, last = outputs(q)
                            v.reciprocal(rden[:, q, 0:n3].rearrange("p (j c) -> p j c", c=HG), first[:, :, :, HD])
                            ins = v.reciprocal(rden[:, q, n3:H], last[:, :, HD])
                        ins.then_inc(dve_den, 1)
                    if n == 9 and has(s, -2):
                        dve.wait_ge(dve_den, upto(fin))
                        dve.wait_ge(pe_oTn, upto(fin + (-1)))
                        for q in range(QT):
                            first, last = outputs(q)
                            rd = rden[:, q, :].unsqueeze(2).to_broadcast([P, H, HD])
                            v.tensor_tensor(o_sb[:, q, 0:n3 * HD].rearrange("p (j c d) -> p j c d", j=VGRP, d=HD),
                                            first[:, :, :, 0:HD],
                                            rd[:, 0:n3, :].rearrange("p (j c) d -> p j c d", c=HG), ALU.mult)
                            ins = v.tensor_tensor(o_sb[:, q, n3 * HD:D].rearrange("p (c d) -> p c d", d=HD),
                                                  last[:, :, 0:HD], rd[:, n3:H, :], ALU.mult)
                        ins.then_inc(dve_o, 1)
                    if n == 9 and has(s, -1):
                        lower_experts(t + (-1), 1)
                    if n == 10 and has(s, 0):
                        gates(t, SHARE)
                    if n == 10 and has(s, 2):
                        nxt = t + 2
                        dve.wait_ge(pool_rstd, upto(nxt))
                        dve.wait_ge(pe_xnT, upto(nxt + (-1)))
                        for q in range(QT):
                            ins = v.tensor_scalar(xn[:, q, :], x_sb[nxt.buf][:, q, :], mv[:, q, 0:1], rstd[:, q:q + 1],
                                                  ALU.subtract, ALU.mult)
                        ins.then_inc(dve_xn, 1)
                if has(s, 0):
                    max_parts(t, 0)
                    gates(t, WEIGHT)
                    for k in range(1, 4):
                        max_parts(t, k)
                if has(s, -2):
                    dve.wait_ge(pe_y, upto(fin))
                    dve.wait_ge(pool_sum, upto(fin, per=RESULT))
                    dve.wait_ge(dma_out, upto(fin + (-1), unit=16))
                    v.tensor_tensor(out_sb[:].rearrange("p q d -> p (q d)"), m0[:, 0:S],
                                    res[:].rearrange("p q d -> p (q d)"), ALU.add).then_inc(dve_out, 1)

            def fill_vaug(b):
                v.memset(vaug[b][:], 0.0).then_inc(dve_zero, 1)
                dve.wait_ge(dve_zero, 2 + b)
                for q in range(QT):
                    vv = vaug[b][:, q].rearrange("p h c -> p (h c)")
                    v.memset(bass.AP(tensor=vv.tensor, offset=vv.offset + HD,
                                     ap=[list(vv.ap[0]), [HG * VW + OW, VGRP], [VW, HG]]), 1.0)
                    ins = v.memset(vaug[b][:, q, n3:H, HD], 1.0)
                ins.then_inc(dve_fill, 1)

            def between(s):
                if s == -2:
                    v.memset(qstack[0][64:MAX_ROW], 0.0)
                    v.memset(kstack[0][64:ALL_ROWS], 1.0).then_inc(dve_fill, 1)
                if s == -1:
                    dve.wait_ge(ld_w, 16 * NW)
                    dve.wait_ge(dve_zero, 1)
                    v.tensor_scalar(bv_wide[:], bv_wide[:], bv_sb[:], None, ALU.add).then_inc(dve_const, 1)
                    fill_vaug(0)
                    dve.wait_ge(pe_bias, 1)
                    dve.wait_ge(ld_bias, 16)
                    v.tensor_tensor(bias_out[:], bias_out[:], m1[:, 0:D], ALU.add).then_inc(dve_bias, 1)
                if 0 <= s < NB - 1:
                    fill_vaug(s + 1)

            v.memset(bv_wide[:], 0.0).then_inc(dve_zero, 1)
            over_slots(dve.Fori, slot, between)

        @block.tensor
        def _(pe):
            tn = nc.tensor

            def score_item(t, n):
                grp, j = n // 3, n % 3
                if n >= 2:
                    pe.wait_ge(dve_max, upto(t, per=ITEMS, k=n - 1))
                else:
                    pe.wait_ge(dve_max, upto(t + (-1), per=ITEMS, k=ITEMS + n - 1))
                if n == 0:
                    pe.wait_ge(dma_stack, upto(t, unit=16 * NSTACK))
                ps = score_ps[n % 2][:]
                qs, ks = qstack[t.buf], kstack[t.buf]
                if j == 0:
                    tn.matmul(ps.rearrange("p (h k) -> p h k", h=HG), ident_b[:],
                              mask_b[:].unsqueeze(1).to_broadcast([P, HG, P]), start=True, stop=False, skip_group_check=True)
                    for c in range(HG):
                        h = HG * grp + c
                        ins = tn.matmul(ps[:, c * P:(c + 1) * P], qs[0:MAX_ROW, h, 0:P], ks[0:MAX_ROW, h, 0:P],
                                        start=False, stop=c == HG - 1, skip_group_check=True)
                else:
                    tn.matmul(ps.rearrange("p (h b k) -> p h b k", h=2, b=2)[:, :, 1, :], ident_b[:],
                              mask_b[:].unsqueeze(1).to_broadcast([P, 2, P]), start=True, stop=False, skip_group_check=True)
                    for c in range(2):
                        h = HG * grp + 2 * (j - 1) + c
                        ins = tn.matmul(ps[:, c * S:(c + 1) * S], qs[0:MAX_ROW, h, P:S], ks[0:MAX_ROW, h, :],
                                        start=False, stop=c == 1, skip_group_check=True)
                ins.then_inc(pe_score, 1)

            def scoreT_item(f, n):
                grp, j = n // 3, n % 3
                if n >= 2:
                    pe.wait_ge(act_exp, upto(f, per=ITEMS, k=n - 1))
                else:
                    pe.wait_ge(act_exp, upto(f + (-1), per=ITEMS, k=ITEMS + n - 1))
                if n == 0:
                    pe.wait_ge(dma_max, upto(f, unit=16))
                ps = scoreT_ps[n % 2][:]
                qs, ks = qstack[f.buf], kstack[f.buf]
                if j < 2:
                    for c in range(2):
                        h = HG * grp + 2 * j + c
                        ins = tn.matmul(ps[:, c * S:(c + 1) * S], ks[0:ALL_ROWS, h, 0:P], qs[0:ALL_ROWS, h, :],
                                        start=True, stop=True)
                else:
                    for c in range(HG):
                        h = HG * grp + c
                        ins = tn.matmul(ps[:, c * P:(c + 1) * P], ks[0:ALL_ROWS, h, P:S], qs[0:ALL_ROWS, h, P:S],
                                        start=True, stop=True)
                ins.then_inc(pe_scoreT, 1)

            def values(f, grp):
                pe.wait_ge(pool_mask, upto(f, per=MASKS, k=2 * grp + 2))
                pe.wait_ge(act_exp, upto(f, per=ITEMS, k=3 * grp + 3))
                if grp == 0:
                    pe.wait_ge(act_v, upto(f))
                    pe.wait_ge(act_oT, upto(f + (-1)))
                pr, va = probs[grp % 2], vaug[f.buf]
                c0 = S if grp == NG - 1 else 0
                for q in range(QT):
                    for c in range(HG):
                        h = HG * grp + c
                        quad = slice(32 * c, 32 * c + 32)
                        o = oT_ps[quad, c0:c0 + S] if q == 0 else oT_ps[quad, c0 + P:c0 + S]
                        i = pr[:, 0:3:2, c, :] if q == 0 else pr[:, 1, c, :]
                        ins = tn.matmul(o, va[:, q, h, :], i, start=q == 0 and grp in (0, NG - 1),
                                        stop=q == 1 and grp in (NG - 2, NG - 1), skip_group_check=True)
                ins.then_inc(pe_pv, 1)

            def experts(m, s, d):
                q, up = d // 2, d % 2
                if d == 0:
                    if has(s, 0):
                        pe.wait_ge(act_v, upto(m + 1))
                    else:
                        pe.wait_ge(dve_lower, upto(m + (-1), per=2))
                if d == 1:
                    if has(s, 1):
                        pe.wait_ge(dve_rest, upto(m + 2, per=2))
                    else:
                        pe.wait_ge(act_upper, upto(m + (-1), per=2))
                if d == 2:
                    pe.wait_ge(dve_lower, upto(m, per=2, k=1))
                if d == 3:
                    pe.wait_ge(act_upper, upto(m, per=2, k=1))
                if s == 1 and d == 0:
                    pe.wait_ge(ld_we, 16)
                tn.matmul(moe_ps[up][:], xnT[m.buf][:, q * P:(q + 1) * P],
                          we_sb[:, EH * up:EH * (up + 1), :].rearrange("p e m -> p (e m)"),
                          start=True, stop=True).then_inc(pe_moe, 1)

            def slot(t, s):
                pre, mix, fin = t + 1, t + (-1), t + (-2)
                for n in range(ITEMS):
                    if has(s, 0):
                        score_item(t, n)
                    if n == 0 and has(s, 0):
                        pe.wait_ge(act_xnT, upto(t))
                        pe.wait_ge(dve_lower, upto(fin, per=2))
                        if s == 0:
                            pe.wait_ge(dve_bias, 1)
                        for q in range(QT):
                            ins = tn.matmul(m1[:, q * VG:(q + 1) * VG], xnT[t.buf][:, q * P:(q + 1) * P], wvg_sb[:],
                                            start=True, stop=True)
                        ins.then_inc(pe_vg, 1)
                    if n == 2 and has(s, 1):
                        pe.wait_ge(act_xnT, upto(pre))
                        for c in range(2):
                            ins = tn.matmul(m2[:, c * S:(c + 1) * S], wqk_sb[:, c, :], xnT[pre.buf][:], start=True, stop=True)
                        ins.then_inc(pe_qk, 1)
                    if n in (3, 5) and has(s, -2):
                        values(fin, (n + 1) // 2)
                    if n in (9, 11) and has(s, -1):
                        values(mix, (n - 9) // 2)
                    if n == 10 and has(s, -2):
                        pe.wait_ge(dve_o, upto(fin))
                        for q in range(QT):
                            ins = tn.transpose(m0[:, q * P:(q + 1) * P], o_sb[:, q, :], ident[:])
                        ins.then_inc(pe_oTn, 1)
                    if n in EXPERT_STEPS and has(s, -1):
                        experts(mix, s, EXPERT_STEPS.index(n))
                    f, k = behind(t, s, n)
                    if f:
                        scoreT_item(f, k)
                    if n == 0 and has(s, 1):
                        pe.wait_ge(dve_xn, upto(pre))
                        pe.wait_ge(act_upper, upto(fin, per=2))
                        for q in range(QT):
                            ins = tn.transpose(m2[:, q * P:(q + 1) * P], xn[:, q, :], ident[:])
                        ins.then_inc(pe_xnT, 1)
                    if n == 1 and has(s, -1):
                        pe.wait_ge(dve_mpart, upto(mix, per=4))
                        pe.wait_ge(dve_out, upto(fin + (-1)))
                        stand_alone(pe, pe_passed)
                        mTp = m0[:].bitcast(BF16)
                        for q in range(QT):
                            ins = tn.transpose(mTp[0:PARTS * H, q * P:(q + 1) * P],
                                               mparts[:, q].rearrange("p a h -> p (a h)"), ident_b[:])
                        ins.then_inc(pe_mT, 1)
                    if n == 7 and has(s, -2):
                        pe.wait_ge(act_oT, upto(fin))
                        if has(s, -1):
                            pe.wait_ge(act_mT, upto(mix))
                        else:
                            pe.wait_ge(dve_out, upto(fin + (-1)))
                        for q in range(QT):
                            for r in range(2):
                                c = (q * 2 + r) * P
                                ins = tn.transpose(m0[:, c:c + P], oT[:, r, q * P:(q + 1) * P], ident[:])
                        ins.then_inc(pe_o, 1)
                    if n == 11 and has(s, -2):
                        pe.wait_ge(act_oTn, upto(fin))
                        for q in range(QT):
                            ins = tn.matmul(m0[:, q * P:(q + 1) * P], oTn[:, q * P:(q + 1) * P], wo_sb[:], start=True, stop=True)
                        ins.then_inc(pe_y, 1)

            def between(s):
                if s == -1:
                    pe.wait_ge(ld_w, 16 * NW)
                    pe.wait_ge(dve_const, 1)
                    tn.matmul(m1[:, 0:D], bv_wide[:], wo_sb[:], start=True, stop=True).then_inc(pe_bias, 1)

            EXPERT_STEPS = (4, 6, 8, 10)
            pe.wait_ge(pool_const, 8)
            pe.wait_ge(ld_qk, 16 * NQK)
            over_slots(pe.Fori, slot, between)


def kernel(L0_attn_x, L0_attn_Wq, L0_attn_bq, L0_attn_Wk, L0_attn_bk, L0_attn_Wv, L0_attn_bv,
           L0_attn_Wo, L0_attn_bo, L0_ffn_gate_w, L0_ffn_We):
    import numpy as np
    import concourse.bacc as bacc
    from concourse.bass_utils import run_bass_kernel_spmd

    def by_feature(w):
        w = np.asarray(w)
        return np.swapaxes(w.reshape((H, HD) + w.shape[1:]), 0, 1).reshape(w.shape)

    host = {
        "x": np.asarray(L0_attn_x).reshape(NSEQ * S, D),
        "wq": by_feature(L0_attn_Wq).T, "wk": by_feature(L0_attn_Wk).T,
        "bq": by_feature(L0_attn_bq), "bk": by_feature(L0_attn_bk),
        "wv": np.asarray(L0_attn_Wv).T, "bv": np.asarray(L0_attn_bv),
        "wo": np.asarray(L0_attn_Wo).T, "bo": np.asarray(L0_attn_bo),
        "gate": np.asarray(L0_ffn_gate_w).T, "we": np.asarray(L0_ffn_We),
    }
    nc = bacc.Bacc("TRN2", target_bir_lowering=False, num_devices=1)
    arrays, args = {}, {}
    for name, a in host.items():
        arrays[f"in_{name}"] = np.ascontiguousarray(a)
        args[name] = nc.dram_tensor(f"in_{name}", a.shape, FP32, kind="ExternalInput").ap()
    out = nc.dram_tensor("out", (NSEQ * S, D), FP32, kind="ExternalOutput").ap()
    bass_block(nc, out=out, **args)
    r = run_bass_kernel_spmd(nc, [arrays], core_ids=[0])
    return r.results[0]["out"].reshape(NSEQ, S, D)
```

```python
from contextlib import ExitStack

import concourse.bass as bass
from concourse import mybir

FP32 = mybir.dt.float32
BF16 = mybir.dt.bfloat16
FP32R = mybir.dt.float32r
U32 = mybir.dt.uint32
ALU = mybir.AluOpType
ACT = mybir.ActivationFunctionType
AX = mybir.AxisListType

NSEQ, S, D = 32, 256, 128
H, HD = 16, 8
E = 8
P = 128
QT = S // P
NB = 3
PARTS = 3
PART_ROWS = PARTS * HD
MAX_ROW = 96
ALL_ROWS = MAX_ROW + PARTS
HG = 4
NG = H // HG
ITEMS = 3 * NG
LAG = 4
VW = 32
VGRP = 3
OW = HD + 1
VG = D + E
EH = 4
MASKS = 2 * NG
SCALE = float(HD) ** -0.5
EPS = 1e-5
MASKED = -3.0e38
HIGH_BITS = 0xFFFFF000
TOP, INDEX, FLOAT, HIT, TOTAL, FIRST, SECOND, SHARE, WEIGHT = range(1, 10)
SUM_Q0, SUM_Q1, PAIRS, FOURS, RESULT = range(1, 6)


def stand_alone(eng, passed):
    eng.sem_inc(passed, 1)


class Seq:

    def __init__(self, i, c):
        self.i, self.c = i, c

    def __add__(self, k):
        return Seq(self.i, self.c + k)

    @property
    def n(self):
        return self.i * NB + self.c

    @property
    def buf(self):
        return self.c % NB

    @property
    def turn(self):
        return self.i + self.c // NB

    @property
    def none(self):
        return isinstance(self.i, int) and self.n < 0


def upto(seq, per=1, k=None, unit=1):
    return 0 if seq.none else (seq.n * per + (per if k is None else k)) * unit


def bass_block(nc, x, wq, wk, bq, bk, wv, bv, wo, bo, gate, we, out):
    ctx = ExitStack()
    with ctx:
        def sb(name, shape, dt=FP32):
            return ctx.enter_context(nc.sbuf_tensor(name, shape, dt))

        def sbs(name, shape, dt=FP32, n=NB):
            return [sb(f"{name}{b}", shape, dt) for b in range(n)]

        def pb(name):
            return ctx.enter_context(nc.psum_tensor(name, [P, 512], FP32))

        def sem(name):
            return ctx.enter_context(nc.semaphore(name))

        def sems(*names):
            return [sem(n) for n in names]

        wqk_sb = sb("wqk_sb", [P, 2, D])
        bqk_sb = sb("bqk_sb", [P, 2])
        wqk_hl = sb("wqk_hl", [P, 2, 2, D], FP32R)
        we_hl = sb("we_hl", [P, 2, E, D], FP32R)
        wvg_sb = sb("wvg_sb", [P, VG])
        wo_sb = sb("wo_sb", [P, D])
        we_sb = sb("we_sb", [P, E, D])
        bv_sb = sb("bv_sb", [P, 1])
        bv_wide = sb("bv_wide", [P, P])
        bias_out = sb("bias_out", [P, D])
        ident = sb("ident", [P, P])
        ident_b = sb("ident_b", [P, P], BF16)
        mask_b = sb("mask_b", [P, P], BF16)
        expert_no = sb("expert_no", [P, E])
        minus_half = sb("minus_half", [P, QT])
        table_load = sb("table_load", [P, QT])
        x_sb = sbs("x_sb", [P, QT, D])
        xb = sbs("xb", [P, QT, D])
        xnT = sbs("xnT", [P, S])
        xnT_hl = sbs("xnT_hl", [P, 2, S], FP32R)
        qstack = sbs("qstack", [P, H, S], BF16)
        kstack = sbs("kstack", [P, H, S], BF16)
        vaug = sbs("vaug", [P, QT, H, VW])
        negmax = sbs("negmax", [P, QT, H])
        weight = sbs("weight", [P, QT, E])
        probs = sbs("probs", [P, 3, HG, P], n=2)
        stats = sb("stats", [P, QT, 6])
        mv = sb("mv", [P, QT, 2])
        var_eps = sb("var_eps", [P, QT])
        rstd = sb("rstd", [P, QT])
        xn = sb("xn", [P, QT, D])
        xnT_high = sb("xnT_high", [P, S])
        w_high = sb("w_high", [P, E, D])
        parts = sb("parts", [P, 2, PARTS, S], BF16)
        rest = sb("rest", [P, 2, S])
        mrest = sb("mrest", [P, QT, H])
        mparts = sb("mparts", [P, QT, PARTS, H], BF16)
        mT = sb("mT", [PARTS * H, S], BF16)
        logits = sb("logits", [P, QT, E])
        top = sb("top", [P, QT, 8])
        topi = sb("topi", [P, QT, 8], U32)
        topf = sb("topf", [P, QT, 2])
        gap = sb("gap", [P, QT])
        egap = sb("egap", [P, QT])
        egap1 = sb("egap1", [P, QT])
        gw = sb("gw", [P, QT, 2])
        hit = sb("hit", [P, QT, 2, E])
        share = sb("share", [P, QT, 2, E])
        lower = sb("lower", [P, EH, QT, D])
        upper = sb("upper", [P, EH, QT, D])
        fours = sb("fours", [P, EH, QT, D])
        pairs = sb("pairs", [P, 2, QT, D])
        mixed = sb("mixed", [P, QT, D])
        out_sb = sb("out_sb", [P, QT, D])
        res = sb("res", [P, QT, D])
        oT = sb("oT", [P, 2, S])
        rden = sb("rden", [P, QT, H])
        o_sb = sb("o_sb", [P, QT, D])
        oTn = sb("oTn", [P, S])

        score_ps = [pb(f"score_ps{b}") for b in range(2)]
        scoreT_ps = [pb(f"scoreT_ps{b}") for b in range(2)]
        oT_ps = pb("oT_ps")
        m0, m1, m2 = pb("m0"), pb("m1"), pb("m2")
        moe_ps = [m1, m2]

        scratch = [nc.dram_tensor(f"scratch{b}", [3 * PARTS - 1, P, S], BF16, kind="Internal").ap() for b in range(NB)]

        ld_qk, ld_w, ld_we, ld_bias, pool_const, dve_const, pe_bias, dve_bias = sems(
            "ld_qk", "ld_w", "ld_we", "ld_bias", "pool_const", "dve_const", "pe_bias", "dve_bias")
        pool_fill, dve_fill, dve_zero, dve_weights, act_weights = sems(
            "pool_fill", "dve_fill", "dve_zero", "dve_weights", "act_weights")
        dma_x = sems(*(f"dma_x{b}" for b in range(NB)))
        dma_scratch_q, dma_scratch_k = sems("dma_scratch_q", "dma_scratch_k")
        dma_stack, dma_max, dma_out = sems("dma_stack", "dma_max", "dma_out")
        dve_stats, dve_mv, pool_eps, pool_rstd, dve_xn = sems("dve_stats", "dve_mv", "pool_eps", "pool_rstd", "dve_xn")
        pe_xnT, act_xnT, dve_halves, act_high, pool_xb = sems("pe_xnT", "act_xnT", "dve_halves", "act_high", "pool_xb")
        pe_qk, act_part1, dve_rest, act_part2, pool_part3 = sems("pe_qk", "act_part1", "dve_rest", "act_part2", "pool_part3")
        pe_score, dve_max, dve_mpart, pe_mT, act_mT = sems("pe_score", "dve_max", "dve_mpart", "pe_mT", "act_mT")
        pe_vg, act_v, dve_gap, act_gate, dve_gate = sems(
            "pe_vg", "act_v", "dve_gap", "act_gate", "dve_gate")
        pe_scoreT, act_exp, pool_mask, pe_pv, act_oT = sems("pe_scoreT", "act_exp", "pool_mask", "pe_pv", "act_oT")
        pe_moe, dve_lower, act_upper, pool_sum = sems("pe_moe", "dve_lower", "act_upper", "pool_sum")
        pe_o, dve_den, dve_o, pe_oTn, act_oTn, pe_y, dve_out = sems(
            "pe_o", "dve_den", "dve_o", "pe_oTn", "act_oTn", "pe_y", "dve_out")
        pool_passed, dve_passed, pe_passed, sp_passed = sems("pool_passed", "dve_passed", "pe_passed", "sp_passed")

        NSTACK = 6
        NQK, NW = 4, 4
        LOOP0 = 3
        LOOPS = (NSEQ - 2 - LOOP0) // NB

        x_t = x.rearrange("(s q p) d -> s p q d", q=QT, p=P)
        out_t = out.rearrange("(s q p) d -> s p q d", q=QT, p=P)

        def over_slots(eng_fori, slot, between=None):
            for s in range(-2, LOOP0):
                slot(Seq(0, s), s)
                if between:
                    between(s)
            with eng_fori(0, LOOPS) as i:
                for u in range(NB):
                    slot(Seq(i, LOOP0 + u), LOOP0 + u)
            for s in range(LOOP0 + NB * LOOPS, NSEQ + 2):
                slot(Seq(0, s), s)

        def has(s, k):
            return 0 <= s + k < NSEQ

        def behind(t, s, n):
            k = -1 if n >= LAG else -2
            return (t + k, (n - LAG) % ITEMS) if has(s, k) else (None, None)

        block = ctx.enter_context(nc.Block())

        @block.sync
        def _(sp):
            sp.dma_start(x_sb[0][:], x_t[0]).then_inc(dma_x[0], 16)
            sp.dma_start(wqk_sb[:, 0, :], wq).then_inc(ld_qk, 16)
            sp.dma_start(wqk_sb[:, 1, :], wk).then_inc(ld_qk, 16)
            sp.dma_start(bqk_sb[:, 0:1], bq.unsqueeze(1)).then_inc(ld_qk, 16)
            sp.dma_start(bqk_sb[:, 1:2], bk.unsqueeze(1)).then_inc(ld_qk, 16)
            sp.dma_start(wvg_sb[:, 0:D], wv).then_inc(ld_w, 16)
            sp.dma_start(wvg_sb[:, D:VG], gate).then_inc(ld_w, 16)
            sp.dma_start(wo_sb[:], wo).then_inc(ld_w, 16)
            sp.dma_start(bv_sb[:], bv.unsqueeze(1)).then_inc(ld_w, 16)
            sp.dma_start(bias_out[:], bo.unsqueeze(0).to_broadcast([P, D])).then_inc(ld_bias, 16)

            def store(fin):
                sp.wait_ge(dve_out, upto(fin))
                sp.dma_start(out_t[fin.n], out_sb[:]).then_inc(dma_out, 16)

            def slot(t, s):
                if has(s, -3):
                    store(t + (-3))
                if has(s, 2) and s > -2:
                    nxt = t + 2
                    sp.wait_ge(dve_xn, upto(nxt + (-NB)))
                    sp.wait_ge(pool_xb, upto(nxt + (-NB)))
                    sp.dma_start(x_sb[nxt.buf][:], x_t[nxt.n]).then_inc(dma_x[nxt.buf], 16)
                if s == -1:
                    sp.dma_start(we_sb[:], we.rearrange("e d m -> d e m")).then_inc(ld_we, 16)
                if has(s, -1):
                    m = t + (-1)
                    sp.wait_ge(act_mT, upto(m))
                    sp.dma_start(qstack[m.buf][MAX_ROW:ALL_ROWS], mT[:]).then_inc(dma_max, 16)
                if has(s, 1):
                    pre, last = t + 1, t + (1 - NB)
                    scr = scratch[pre.buf]
                    sp.wait_ge(act_part1, upto(pre))
                    sp.wait_ge(act_part2, upto(pre, per=2))
                    sp.dma_start(scr[2 * PARTS:].rearrange("a r t -> r a t"), parts[:, 1, 0:PARTS - 1]).then_inc(dma_scratch_k, 16)
                    sp.wait_ge(pool_part3, upto(pre, per=2, k=1))
                    sp.dma_start(scr[0:PARTS].rearrange("a r t -> r a t"), parts[:, 0]).then_inc(dma_scratch_q, 16)
                    sp.wait_ge(pool_part3, upto(pre, per=2))
                    sp.dma_start(scr[PARTS:2 * PARTS].rearrange("a r t -> r a t"), parts[:, 1]).then_inc(dma_scratch_k, 16)
                    sp.wait_ge(pe_scoreT, upto(last, per=ITEMS))
                    sp.wait_ge(pe_score, upto(last, per=ITEMS))
                    stand_alone(sp, sp_passed)
                    if s < 2:
                        sp.wait_ge(dve_fill, 1)
                        sp.wait_ge(pool_fill, 2 * (s + 1) + 1)
                    rows = scr.rearrange("a (d h) t -> (a d) (h t)", h=H)
                    qs, ks = (st[pre.buf][:].rearrange("p h t -> p (h t)") for st in (qstack, kstack))
                    sp.wait_ge(dma_scratch_q, upto(pre, unit=16))
                    for r in range(PARTS):
                        sp.dma_start(qs[r * PART_ROWS:(r + 1) * PART_ROWS], rows[0:PART_ROWS]).then_inc(dma_stack, 16)
                    sp.wait_ge(dma_scratch_k, upto(pre, per=2, unit=16))
                    for r in range(PARTS):
                        turned = PART_ROWS + r * HD
                        sp.dma_start(ks[r * PART_ROWS:(r + 1) * PART_ROWS],
                                     rows[turned:turned + PART_ROWS]).then_inc(dma_stack, 16)

            over_slots(sp.Fori, slot)
            store(Seq(0, NSEQ - 1))
            sp.wait_ge(dma_out, upto(Seq(0, NSEQ - 1), unit=16))

        @block.gpsimd
        def _(pool):
            g = nc.gpsimd
            g.memset(minus_half[:], -0.5).then_inc(pool_const, 1)
            g.memset(ident[:], 0.0).then_inc(pool_const, 1)
            g.memset(ident_b[:], 0.0).then_inc(pool_const, 1)
            g.memset(mask_b[:], 0.0).then_inc(pool_const, 1)
            g.iota(expert_no[:], pattern=[[1, E]], base=0, channel_multiplier=0,
                   allow_small_or_imprecise_dtypes=True).then_inc(pool_const, 1)
            pool.wait_ge(pool_const, 5)
            for m in (ident, ident_b):
                g.affine_select(out=m[:], in_=m[:], compare_op=ALU.not_equal, fill=1.0, base=0,
                                pattern=[[-1, P]], channel_multiplier=1).then_inc(pool_const, 1)
            g.affine_select(out=mask_b[:], in_=mask_b[:], compare_op=ALU.is_ge, fill=MASKED, base=0,
                            pattern=[[-1, P]], channel_multiplier=1).then_inc(pool_const, 1)

            def mask(f, grp, block_no):
                k = 3 * grp + 2 + block_no
                pool.wait_ge(act_exp, upto(f, per=ITEMS, k=k))
                stand_alone(pool, pool_passed)
                pr = probs[grp % 2][:, block_no]
                g.affine_select(out=pr, in_=pr, compare_op=ALU.is_ge, fill=0.0, base=0,
                                pattern=[[0, HG], [1, P]], channel_multiplier=-1).then_inc(pool_mask, 1)

            def part3(pre, c):
                pool.wait_ge(act_part2, upto(pre, per=2, k=c + 1))
                pool.wait_ge(dma_scratch_q, upto(pre + (-1), unit=16))
                pool.wait_ge(dma_scratch_k, upto(pre + (-1), per=2, unit=16))
                g.tensor_tensor(parts[:, c, 2, :], rest[:, c, :], parts[:, c, 1, :], ALU.subtract).then_inc(pool_part3, 1)

            def sum_tile(m, q):
                pool.wait_ge(dve_lower, upto(m, per=2, k=q + 1))
                pool.wait_ge(act_upper, upto(m, per=2, k=q + 1))
                g.tensor_tensor(fours[:, :, q, :], lower[:, :, q, :], upper[:, :, q, :], ALU.add).then_inc(pool_sum, 1)

            def slot(t, s):
                for n in range(ITEMS):
                    f, k = behind(t, s, n)
                    if f and k % 3:
                        mask(f, k // 3, k % 3 - 1)
                    if n == (1 if has(s, -1) else 3) and has(s, -2):
                        sum_tile(t + (-2), 1)
                    if n == 3 and has(s, 1):
                        part3(t + 1, 0)
                        part3(t + 1, 1)
                    if n == 4 and has(s, -2):
                        m = t + (-2)
                        pool.wait_ge(pool_sum, upto(m, per=RESULT, k=SUM_Q1))
                        g.tensor_tensor(pairs[:], fours[:, 0:2], fours[:, 2:4], ALU.add).then_inc(pool_sum, 1)
                    if n == 6 and has(s, -2):
                        m = t + (-2)
                        pool.wait_ge(pool_sum, upto(m, per=RESULT, k=PAIRS))
                        g.tensor_tensor(mixed[:], pairs[:, 0], pairs[:, 1], ALU.add).then_inc(pool_sum, 1)
                    if n == 7 and has(s, 2):
                        nxt = t + 2
                        pool.wait_ge(dve_mv, upto(nxt))
                        pool.wait_ge(dve_xn, upto(nxt + (-1)))
                        stand_alone(pool, pool_passed)
                        g.tensor_scalar(var_eps[:], mv[:, :, 1], 1.0, EPS, ALU.mult, ALU.add).then_inc(pool_eps, 1)
                        pool.wait_ge(pool_eps, upto(nxt))
                        g.tensor_tensor(rstd[:], var_eps[:], minus_half[:], ALU.pow).then_inc(pool_rstd, 1)
                    if n == 8 and has(s, -2):
                        m = t + (-2)
                        pool.wait_ge(pool_sum, upto(m, per=RESULT, k=FOURS))
                        pool.wait_ge(pool_xb, upto(m))
                        pool.wait_ge(dve_out, upto(m + (-1)))
                        g.tensor_tensor(res[:], mixed[:], xb[m.buf][:], ALU.add).then_inc(pool_sum, 1)
                    if n == 9 and has(s, 0):
                        pool.wait_ge(dma_x[t.buf], 16 * (t.turn + 1))
                        if s == 0:
                            pool.wait_ge(dve_bias, 1)
                        g.tensor_tensor(xb[t.buf][:], x_sb[t.buf][:],
                                        bias_out[:].unsqueeze(1).to_broadcast([P, QT, D]), ALU.add).then_inc(pool_xb, 1)
                    if n == 10 and has(s, -1):
                        sum_tile(t + (-1), 0)

            def between(s):
                if s == -2:
                    g.memset(kstack[0][:], 1.0).then_inc(pool_fill, 1)
                elif s < NB - 2:
                    g.memset(qstack[s + 2][:], 0.0).then_inc(pool_fill, 1)
                    g.memset(kstack[s + 2][:], 1.0).then_inc(pool_fill, 1)

            over_slots(pool.Fori, slot, between)

        @block.scalar
        def _(act):
            a = nc.scalar

            def take_exp(f, k):
                grp, j = k // 3, k % 3
                pr = probs[grp % 2]
                act.wait_ge(pe_scoreT, upto(f, per=ITEMS, k=k + 1))
                if j == 0:
                    if grp >= 2:
                        act.wait_ge(pe_pv, upto(f, per=NG, k=grp - 1))
                    else:
                        act.wait_ge(pe_pv, upto(f + (-1), per=NG, k=NG + grp - 1))
                if j < 2:
                    o = pr[:, 0:3:2, 2 * j:2 * j + 2, :].rearrange("p b h c -> p h b c")
                    i = scoreT_ps[k % 2][:].rearrange("p (h b c) -> p h b c", h=2, b=2)
                else:
                    o = pr[:, 1]
                    i = scoreT_ps[k % 2][:].rearrange("p (h q) -> p h q", h=HG)
                a.activation(o, i, ACT.Exp, scale=SCALE).then_inc(act_exp, 1)

            def take_values(t, s):
                act.wait_ge(pe_vg, upto(t))
                act.wait_ge(dve_gate, upto(t + (-1), per=WEIGHT, k=INDEX))
                a.copy(logits[:], m1[:, 0:QT * VG].rearrange("p (q c) -> p q c", q=QT)[:, :, D:VG])
                act.wait_ge(pe_pv, upto(t + (-NB), per=NG))
                if s < NB:
                    act.wait_ge(dve_fill, 2 + s)
                for q in range(QT):
                    v = vaug[t.buf][:, q].rearrange("p h c -> p (h c)")
                    src = m1[:, q * VG:q * VG + D]
                    n3 = VGRP * HG
                    dst = bass.AP(tensor=v.tensor, offset=v.offset,
                                  ap=[list(v.ap[0]), [HG * VW + OW, VGRP], [VW, HG], [1, HD]])
                    a.copy(dst, src[:, 0:n3 * HD].rearrange("p (j c d) -> p j c d", j=VGRP, d=HD))
                    ins = a.copy(vaug[t.buf][:, q, n3:H, 0:HD], src[:, n3 * HD:D].rearrange("p (c d) -> p c d", d=HD))
                ins.then_inc(act_v, 1)

            def part1(pre):
                act.wait_ge(pe_qk, upto(pre))
                act.wait_ge(dma_scratch_q, upto(pre + (-1), unit=16))
                act.wait_ge(dma_scratch_k, upto(pre + (-1), per=2, unit=16))
                for c in range(2):
                    ins = a.activation(parts[:, c, 0, :], m2[:, c * S:(c + 1) * S], ACT.Identity, bias=bqk_sb[:, c:c + 1])
                ins.then_inc(act_part1, 1)

            def part2(pre, c):
                act.wait_ge(dve_rest, upto(pre, per=2, k=c + 1))
                a.copy(parts[:, c, 1, :], rest[:, c, :]).then_inc(act_part2, 1)

            def upper_experts(m, q):
                act.wait_ge(pe_moe, upto(m, per=4, k=2 * q + 2))
                act.wait_ge(dve_gate, upto(m, per=WEIGHT))
                act.wait_ge(pool_sum, upto(m + (-1), per=RESULT, k=q + 1))
                for e in range(EH):
                    ins = a.activation(upper[:, e, q, :], m2[:, e * D:(e + 1) * D], ACT.Copy,
                                       scale=weight[m.buf][:, q, EH + e:EH + e + 1])
                ins.then_inc(act_upper, 1)

            def slot(t, s):
                for n in range(ITEMS):
                    if n == 1 and has(s, -1):
                        m = t + (-1)
                        act.wait_ge(pe_mT, upto(m))
                        act.wait_ge(dma_max, upto(m + (-1), unit=16))
                        a.copy(mT[:], m0[:].bitcast(BF16)[0:PARTS * H, 0:S]).then_inc(act_mT, 1)
                    if n == 1 and has(s, 1):
                        part1(t + 1)
                    if n == 0 and has(s, 1):
                        act.wait_ge(dve_halves, upto(t + 1, per=2, k=1))
                        act.wait_ge(pe_moe, upto(t + (1 - NB), per=4))
                        a.copy(xnT_hl[(t + 1).buf][:, 0], xnT_high[:]).then_inc(act_high, 1)
                    if n == 0 and has(s, 0):
                        take_values(t, s)
                    if n == 11 and has(s, 2):
                        nxt = t + 2
                        act.wait_ge(pe_xnT, upto(nxt))
                        act.wait_ge(pe_moe, upto(nxt + (-NB), per=4))
                        a.copy(xnT[nxt.buf][:], m1[:, 0:S]).then_inc(act_xnT, 1)
                    if n == 11 and has(s, -1):
                        upper_experts(t + (-1), 1)
                    f, k = behind(t, s, n)
                    if f:
                        take_exp(f, k)
                    if n in (2, 3) and has(s, 1):
                        part2(t + 1, n - 2)
                    if n == 5 and has(s, -2):
                        fin = t + (-2)
                        act.wait_ge(pe_pv, upto(fin, per=NG))
                        act.wait_ge(pe_o, upto(fin + (-1)))
                        a.copy(oT[:].rearrange("p r t -> p (r t)"), oT_ps[:]).then_inc(act_oT, 1)
                    if n == 5 and has(s, 0):
                        act.wait_ge(dve_gap, upto(t))
                        a.activation(egap[:], gap[:], ACT.Exp).then_inc(act_gate, 1)
                    if n == 10 and has(s, -2):
                        fin = t + (-2)
                        act.wait_ge(pe_oTn, upto(fin))
                        act.wait_ge(pe_y, upto(fin + (-1)))
                        a.copy(oTn[:], m0[:, 0:S]).then_inc(act_oTn, 1)
                    if n == 6 and has(s, -1):
                        upper_experts(t + (-1), 0)

            def between(s):
                if s == 0:
                    act.wait_ge(dve_weights, 3)
                    a.copy(we_hl[:, 0], w_high[:]).then_inc(act_weights, 1)

            act.wait_ge(pool_const, 1)
            a.activation(table_load[:], minus_half[:], ACT.Exp)
            act.wait_ge(ld_qk, 16 * NQK)
            act.wait_ge(dve_weights, 1)
            a.copy(wqk_hl[:, 0], w_high[:, 0:2]).then_inc(act_weights, 1)
            over_slots(act.Fori, slot, between)

        @block.vector
        def _(dve):
            v = nc.vector
            n3 = VGRP * HG

            def take_max(t, n):
                dve.wait_ge(pe_score, upto(t, per=ITEMS, k=n + 1))
                grp, j = n // 3, n % 3
                if j == 0:
                    o, w = negmax[t.buf][:, 0, HG * grp:HG * grp + HG], HG
                else:
                    h0 = HG * grp + 2 * (j - 1)
                    o, w = negmax[t.buf][:, 1, h0:h0 + 2], 2
                v.tensor_reduce(o, score_ps[n % 2][:].rearrange("p (h k) -> p h k", h=w),
                                axis=AX.X, op=ALU.max, negate=True).then_inc(dve_max, 1)

            def gates(t, k):
                if k == TOP:
                    dve.wait_ge(act_v, upto(t))
                    stand_alone(dve, dve_passed)
                    for q in range(QT):
                        ins = v.max(top[:, q, :], logits[:, q, :])
                if k == INDEX:
                    dve.wait_ge(dve_gate, upto(t, per=WEIGHT, k=TOP))
                    v.tensor_tensor(gap[:], top[:, :, 1], top[:, :, 0], ALU.subtract).then_inc(dve_gap, 1)
                    for q in range(QT):
                        ins = v.max_index(topi[:, q, :], top[:, q, :], logits[:, q, :])
                if k == FLOAT:
                    dve.wait_ge(dve_gate, upto(t, per=WEIGHT, k=INDEX))
                    ins = v.tensor_copy(topf[:], topi[:, :, 0:2])
                if k == HIT:
                    dve.wait_ge(dve_gate, upto(t, per=WEIGHT, k=FLOAT))
                    ins = v.tensor_tensor(hit[:], expert_no[:].unsqueeze(1).unsqueeze(1).to_broadcast([P, QT, 2, E]),
                                          topf[:].unsqueeze(3).to_broadcast([P, QT, 2, E]), ALU.is_equal)
                if k == TOTAL:
                    dve.wait_ge(act_gate, upto(t))
                    ins = v.tensor_scalar(egap1[:], egap[:], 1.0, None, ALU.add)
                if k == FIRST:
                    dve.wait_ge(dve_gate, upto(t, per=WEIGHT, k=TOTAL))
                    ins = v.reciprocal(gw[:, :, 0], egap1[:])
                if k == SECOND:
                    dve.wait_ge(dve_gate, upto(t, per=WEIGHT, k=FIRST))
                    ins = v.tensor_tensor(gw[:, :, 1], egap[:], gw[:, :, 0], ALU.mult)
                if k == SHARE:
                    dve.wait_ge(dve_gate, upto(t, per=WEIGHT, k=SECOND))
                    ins = v.tensor_tensor(share[:], hit[:], gw[:].unsqueeze(3).to_broadcast([P, QT, 2, E]), ALU.mult)
                if k == WEIGHT:
                    dve.wait_ge(dve_gate, upto(t, per=WEIGHT, k=SHARE))
                    dve.wait_ge(pe_moe, upto(t + (-NB), per=4))
                    ins = v.tensor_tensor(weight[t.buf][:], share[:, :, 0], share[:, :, 1], ALU.add)
                ins.then_inc(dve_gate, 1)

            def lower_experts(m, q):
                dve.wait_ge(pe_moe, upto(m, per=4, k=2 * q + 1))
                dve.wait_ge(dve_gate, upto(m, per=WEIGHT))
                dve.wait_ge(pool_sum, upto(m + (-1), per=RESULT, k=q + 1))
                v.tensor_tensor(lower[:, :, q, :], m1[:].rearrange("p (e m) -> p e m", e=EH),
                                weight[m.buf][:, q, 0:EH].unsqueeze(2).to_broadcast([P, EH, D]),
                                ALU.mult).then_inc(dve_lower, 1)

            def max_parts(t, k):
                if k == 0:
                    dve.wait_ge(dve_max, upto(t, per=ITEMS))
                    dve.wait_ge(pe_mT, upto(t + (-1)))
                    ins = v.tensor_copy(mparts[:, :, 0, :], negmax[t.buf][:])
                else:
                    dve.wait_ge(dve_mpart, upto(t, per=4, k=k))
                if k == 1:
                    ins = v.tensor_tensor(mrest[:], negmax[t.buf][:], mparts[:, :, 0, :], ALU.subtract)
                if k == 2:
                    ins = v.tensor_copy(mparts[:, :, 1, :], mrest[:])
                if k == 3:
                    ins = v.tensor_tensor(mparts[:, :, 2, :], mrest[:], mparts[:, :, 1, :], ALU.subtract)
                ins.then_inc(dve_mpart, 1)

            def outputs(q):
                o4 = m0[:].rearrange("p (q r c w) -> p q r c w", q=QT, r=2, c=HG)
                return o4[:, q, 0, :, 0:VGRP * OW].rearrange("p c (j w) -> p j c w", w=OW), o4[:, q, 1, :, 0:OW]

            def high_half(full, high):
                return v.tensor_scalar(high.bitcast(U32), full.bitcast(U32), HIGH_BITS, None, ALU.bitwise_and)

            def low_half(full, high, low):
                return v.tensor_tensor(low, full, high, ALU.subtract)

            def halve_input(nxt, k):
                if k == 0:
                    dve.wait_ge(act_xnT, upto(nxt))
                    dve.wait_ge(act_high, upto(nxt + (-1)))
                    high_half(xnT[nxt.buf][:], xnT_high[:]).then_inc(dve_halves, 1)
                else:
                    dve.wait_ge(dve_halves, upto(nxt, per=2, k=1))
                    dve.wait_ge(pe_moe, upto(nxt + (-NB), per=4))
                    low_half(xnT[nxt.buf][:], xnT_high[:], xnT_hl[nxt.buf][:, 1]).then_inc(dve_halves, 1)

            def slot(t, s):
                fin = t + (-2)
                for n in range(ITEMS):
                    if has(s, 0):
                        take_max(t, n)
                    if n == 1 and has(s, 0):
                        gates(t, TOP)
                    if n == 2 and has(s, 1):
                        pre = t + 1
                        dve.wait_ge(act_part1, upto(pre))
                        dve.wait_ge(pool_part3, upto(pre + (-1), per=2))
                        for c in range(2):
                            v.scalar_tensor_tensor(rest[:, c, :], m2[:, c * S:(c + 1) * S], bqk_sb[:, c:c + 1],
                                                   parts[:, c, 0, :], ALU.add, ALU.subtract).then_inc(dve_rest, 1)
                    if n == 4 and has(s, 0):
                        gates(t, INDEX)
                    if n == 5 and has(s, 0):
                        gates(t, FLOAT)
                    if n == 5 and has(s, -1):
                        lower_experts(t + (-1), 0)
                    if n == 6 and has(s, 0):
                        gates(t, HIT)
                        gates(t, TOTAL)
                    if n == 6 and has(s, 2):
                        nxt = t + 2
                        dve.wait_ge(dma_x[nxt.buf], 16 * (nxt.turn + 1))
                        for q in range(QT):
                            ins = v.bn_stats(stats[:, q, :], x_sb[nxt.buf][:, q, :])
                        ins.then_inc(dve_stats, 1)
                    if n == 7 and has(s, 2):
                        nxt = t + 2
                        dve.wait_ge(dve_stats, upto(nxt))
                        dve.wait_ge(pool_eps, upto(nxt + (-1)))
                        stand_alone(dve, dve_passed)
                        for q in range(QT):
                            ins = v.bn_aggr(mv[:, q, :], stats[:, q, :])
                        ins.then_inc(dve_mv, 1)
                    if n == 7 and s == -2:
                        dve.wait_ge(ld_qk, 16 * NQK)
                        high_half(wqk_sb[:], w_high[:, 0:2]).then_inc(dve_weights, 1)
                        dve.wait_ge(dve_weights, 1)
                        low_half(wqk_sb[:], w_high[:, 0:2], wqk_hl[:, 1]).then_inc(dve_weights, 1)
                    if n == 7 and has(s, 0):
                        gates(t, FIRST)
                    if n == 8 and has(s, 0):
                        gates(t, SECOND)
                    if n == 8 and has(s, -2):
                        dve.wait_ge(pe_o, upto(fin))
                        for q in range(QT):
                            first, last = outputs(q)
                            v.reciprocal(rden[:, q, 0:n3].rearrange("p (j c) -> p j c", c=HG), first[:, :, :, HD])
                            ins = v.reciprocal(rden[:, q, n3:H], last[:, :, HD])
                        ins.then_inc(dve_den, 1)
                    if n == 9 and has(s, -2):
                        dve.wait_ge(dve_den, upto(fin))
                        dve.wait_ge(pe_oTn, upto(fin + (-1)))
                        for q in range(QT):
                            first, last = outputs(q)
                            rd = rden[:, q, :].unsqueeze(2).to_broadcast([P, H, HD])
                            v.tensor_tensor(o_sb[:, q, 0:n3 * HD].rearrange("p (j c d) -> p j c d", j=VGRP, d=HD),
                                            first[:, :, :, 0:HD],
                                            rd[:, 0:n3, :].rearrange("p (j c) d -> p j c d", c=HG), ALU.mult)
                            ins = v.tensor_tensor(o_sb[:, q, n3 * HD:D].rearrange("p (c d) -> p c d", d=HD),
                                                  last[:, :, 0:HD], rd[:, n3:H, :], ALU.mult)
                        ins.then_inc(dve_o, 1)
                    if n == 9 and has(s, 2):
                        nxt = t + 2
                        dve.wait_ge(pool_rstd, upto(nxt))
                        dve.wait_ge(pe_xnT, upto(nxt + (-1)))
                        for q in range(QT):
                            ins = v.tensor_scalar(xn[:, q, :], x_sb[nxt.buf][:, q, :], mv[:, q, 0:1], rstd[:, q:q + 1],
                                                  ALU.subtract, ALU.mult)
                        ins.then_inc(dve_xn, 1)
                    if n == 9 and has(s, -1):
                        lower_experts(t + (-1), 1)
                    if n == 10 and has(s, 0):
                        gates(t, SHARE)
                if has(s, 0):
                    max_parts(t, 0)
                    gates(t, WEIGHT)
                    max_parts(t, 1)
                if has(s, 2):
                    halve_input(t + 2, 0)
                if has(s, 0):
                    max_parts(t, 2)
                if has(s, 2):
                    halve_input(t + 2, 1)
                if has(s, 0):
                    max_parts(t, 3)
                if has(s, -2):
                    dve.wait_ge(pe_y, upto(fin))
                    dve.wait_ge(pool_sum, upto(fin, per=RESULT))
                    dve.wait_ge(dma_out, upto(fin + (-1), unit=16))
                    v.tensor_tensor(out_sb[:].rearrange("p q d -> p (q d)"), m0[:, 0:S],
                                    res[:].rearrange("p q d -> p (q d)"), ALU.add).then_inc(dve_out, 1)

            def fill_vaug(b):
                v.memset(vaug[b][:], 0.0).then_inc(dve_zero, 1)
                dve.wait_ge(dve_zero, 2 + b)
                for q in range(QT):
                    vv = vaug[b][:, q].rearrange("p h c -> p (h c)")
                    v.memset(bass.AP(tensor=vv.tensor, offset=vv.offset + HD,
                                     ap=[list(vv.ap[0]), [HG * VW + OW, VGRP], [VW, HG]]), 1.0)
                    ins = v.memset(vaug[b][:, q, n3:H, HD], 1.0)
                ins.then_inc(dve_fill, 1)

            def between(s):
                if s == -1:
                    dve.wait_ge(ld_w, 16 * NW)
                    dve.wait_ge(dve_zero, 1)
                    v.tensor_scalar(bv_wide[:], bv_wide[:], bv_sb[:], None, ALU.add).then_inc(dve_const, 1)
                    fill_vaug(0)
                    dve.wait_ge(pe_bias, 1)
                    dve.wait_ge(ld_bias, 16)
                    v.tensor_tensor(bias_out[:], bias_out[:], m0[:, 0:D], ALU.add).then_inc(dve_bias, 1)
                if 0 <= s < NB - 1:
                    fill_vaug(s + 1)
                if s == 0:
                    dve.wait_ge(ld_we, 16)
                    dve.wait_ge(act_weights, 1)
                    high_half(we_sb[:], w_high[:]).then_inc(dve_weights, 1)
                    dve.wait_ge(dve_weights, 3)
                    low_half(we_sb[:], w_high[:], we_hl[:, 1]).then_inc(dve_weights, 1)

            v.memset(bv_wide[:], 0.0).then_inc(dve_zero, 1)
            v.memset(qstack[0][64:MAX_ROW], 0.0).then_inc(dve_fill, 1)
            over_slots(dve.Fori, slot, between)

        @block.tensor
        def _(pe):
            tn = nc.tensor

            def by_halves(o, high, low, other_high, other_low):
                for first, l, r in ((True, high, other_high), (False, high, other_low), (False, low, other_high)):
                    ins = tn.matmul(o, l, r, start=first, stop=l is low)
                return ins

            def score_item(t, n):
                grp, j = n // 3, n % 3
                if n >= 2:
                    pe.wait_ge(dve_max, upto(t, per=ITEMS, k=n - 1))
                else:
                    pe.wait_ge(dve_max, upto(t + (-1), per=ITEMS, k=ITEMS + n - 1))
                if n == 0:
                    pe.wait_ge(dma_stack, upto(t, unit=16 * NSTACK))
                ps = score_ps[n % 2][:]
                qs, ks = qstack[t.buf], kstack[t.buf]
                if j == 0:
                    tn.matmul(ps.rearrange("p (h k) -> p h k", h=HG), ident_b[:],
                              mask_b[:].unsqueeze(1).to_broadcast([P, HG, P]), start=True, stop=False, skip_group_check=True)
                    for c in range(HG):
                        h = HG * grp + c
                        ins = tn.matmul(ps[:, c * P:(c + 1) * P], qs[0:MAX_ROW, h, 0:P], ks[0:MAX_ROW, h, 0:P],
                                        start=False, stop=c == HG - 1, skip_group_check=True)
                else:
                    tn.matmul(ps.rearrange("p (h b k) -> p h b k", h=2, b=2)[:, :, 1, :], ident_b[:],
                              mask_b[:].unsqueeze(1).to_broadcast([P, 2, P]), start=True, stop=False, skip_group_check=True)
                    for c in range(2):
                        h = HG * grp + 2 * (j - 1) + c
                        ins = tn.matmul(ps[:, c * S:(c + 1) * S], qs[0:MAX_ROW, h, P:S], ks[0:MAX_ROW, h, :],
                                        start=False, stop=c == 1, skip_group_check=True)
                ins.then_inc(pe_score, 1)

            def scoreT_item(f, n):
                grp, j = n // 3, n % 3
                if n >= 2:
                    pe.wait_ge(act_exp, upto(f, per=ITEMS, k=n - 1))
                else:
                    pe.wait_ge(act_exp, upto(f + (-1), per=ITEMS, k=ITEMS + n - 1))
                if n == 0:
                    pe.wait_ge(dma_max, upto(f, unit=16))
                ps = scoreT_ps[n % 2][:]
                qs, ks = qstack[f.buf], kstack[f.buf]
                if j < 2:
                    for c in range(2):
                        h = HG * grp + 2 * j + c
                        ins = tn.matmul(ps[:, c * S:(c + 1) * S], ks[0:ALL_ROWS, h, 0:P], qs[0:ALL_ROWS, h, :],
                                        start=True, stop=True)
                else:
                    for c in range(HG):
                        h = HG * grp + c
                        ins = tn.matmul(ps[:, c * P:(c + 1) * P], ks[0:ALL_ROWS, h, P:S], qs[0:ALL_ROWS, h, P:S],
                                        start=True, stop=True)
                ins.then_inc(pe_scoreT, 1)

            def values(f, grp):
                pe.wait_ge(pool_mask, upto(f, per=MASKS, k=2 * grp + 2))
                pe.wait_ge(act_exp, upto(f, per=ITEMS, k=3 * grp + 3))
                if grp == 0:
                    pe.wait_ge(act_v, upto(f))
                    pe.wait_ge(act_oT, upto(f + (-1)))
                pr, va = probs[grp % 2], vaug[f.buf]
                c0 = S if grp == NG - 1 else 0
                for q in range(QT):
                    for c in range(HG):
                        h = HG * grp + c
                        quad = slice(32 * c, 32 * c + 32)
                        o = oT_ps[quad, c0:c0 + S] if q == 0 else oT_ps[quad, c0 + P:c0 + S]
                        i = pr[:, 0:3:2, c, :] if q == 0 else pr[:, 1, c, :]
                        ins = tn.matmul(o, va[:, q, h, :], i, start=q == 0 and grp in (0, NG - 1),
                                        stop=q == 1 and grp in (NG - 2, NG - 1), skip_group_check=True)
                ins.then_inc(pe_pv, 1)

            def experts(m, s, d):
                q, up = d // 2, d % 2
                if d == 0:
                    if has(s, 0):
                        pe.wait_ge(act_v, upto(m + 1))
                    else:
                        pe.wait_ge(dve_lower, upto(m + (-1), per=2))
                if d == 1:
                    if has(s, 1):
                        pe.wait_ge(dve_rest, upto(m + 2, per=2))
                    else:
                        pe.wait_ge(act_upper, upto(m + (-1), per=2))
                if d == 2:
                    pe.wait_ge(dve_lower, upto(m, per=2, k=1))
                if d == 3:
                    pe.wait_ge(act_upper, upto(m, per=2, k=1))
                if s == 1 and d == 0:
                    pe.wait_ge(dve_weights, 4)
                    pe.wait_ge(act_weights, 2)
                cols = slice(q * P, (q + 1) * P)
                by_halves(moe_ps[up][:], xnT_hl[m.buf][:, 0, cols], xnT_hl[m.buf][:, 1, cols],
                          *(we_hl[:, a, EH * up:EH * (up + 1), :].rearrange("p e m -> p (e m)") for a in range(2))
                          ).then_inc(pe_moe, 1)

            def slot(t, s):
                pre, mix, fin = t + 1, t + (-1), t + (-2)
                for n in range(ITEMS):
                    f, k = behind(t, s, n)
                    if has(s, 0):
                        score_item(t, n)
                    elif f:
                        scoreT_item(f, k)
                    if n == 11 and has(s, 2):
                        pe.wait_ge(dve_xn, upto(t + 2))
                        if has(s, -1):
                            pe.wait_ge(dve_lower, upto(mix, per=2))
                        elif has(s, 0):
                            pe.wait_ge(act_v, upto(t))
                        for q in range(QT):
                            ins = tn.transpose(m1[:, q * P:(q + 1) * P], xn[:, q, :], ident[:])
                        ins.then_inc(pe_xnT, 1)
                    if n == 0 and has(s, 0):
                        if has(s, 1):
                            pe.wait_ge(act_xnT, upto(pre))
                        else:
                            pe.wait_ge(dve_lower, upto(fin, per=2))
                        for q in range(QT):
                            ins = tn.matmul(m1[:, q * VG:(q + 1) * VG], xnT[t.buf][:, q * P:(q + 1) * P], wvg_sb[:],
                                            start=True, stop=True)
                        ins.then_inc(pe_vg, 1)
                    if n == 1 and has(s, -1):
                        pe.wait_ge(dve_mpart, upto(mix, per=4))
                        if s == 1:
                            pe.wait_ge(dve_bias, 1)
                        pe.wait_ge(dve_out, upto(fin + (-1)))
                        stand_alone(pe, pe_passed)
                        mTp = m0[:].bitcast(BF16)
                        for q in range(QT):
                            ins = tn.transpose(mTp[0:PARTS * H, q * P:(q + 1) * P],
                                               mparts[:, q].rearrange("p a h -> p (a h)"), ident_b[:])
                        ins.then_inc(pe_mT, 1)
                    if n == 3 and has(s, -2):
                        values(fin, NG - 2)
                    if n in (9, 11) and has(s, -1):
                        values(mix, (n - 9) // 2)
                    if n in EXPERT_STEPS and has(s, -1):
                        experts(mix, s, EXPERT_STEPS.index(n))
                    if n == 10 and has(s, -2):
                        pe.wait_ge(dve_o, upto(fin))
                        for q in range(QT):
                            ins = tn.transpose(m0[:, q * P:(q + 1) * P], o_sb[:, q, :], ident[:])
                        ins.then_inc(pe_oTn, 1)
                    if f and has(s, 0):
                        scoreT_item(f, k)
                    if n == 5 and has(s, -2):
                        values(fin, NG - 1)
                    if n == 1 and has(s, 1):
                        pe.wait_ge(act_upper, upto(fin, per=2))
                        pe.wait_ge(dve_halves, upto(pre, per=2))
                        pe.wait_ge(act_high, upto(pre))
                        if s == -1:
                            pe.wait_ge(dve_weights, 2)
                            pe.wait_ge(act_weights, 1)
                        for c in range(2):
                            ins = by_halves(m2[:, c * S:(c + 1) * S], wqk_hl[:, 0, c], wqk_hl[:, 1, c],
                                            xnT_hl[pre.buf][:, 0], xnT_hl[pre.buf][:, 1])
                        ins.then_inc(pe_qk, 1)
                    if n == 7 and has(s, -2):
                        pe.wait_ge(act_oT, upto(fin))
                        if has(s, -1):
                            pe.wait_ge(act_mT, upto(mix))
                        else:
                            pe.wait_ge(dve_out, upto(fin + (-1)))
                        for q in range(QT):
                            for r in range(2):
                                c = (q * 2 + r) * P
                                ins = tn.transpose(m0[:, c:c + P], oT[:, r, q * P:(q + 1) * P], ident[:])
                        ins.then_inc(pe_o, 1)
                    if n == 11 and has(s, -2):
                        pe.wait_ge(act_oTn, upto(fin))
                        for q in range(QT):
                            ins = tn.matmul(m0[:, q * P:(q + 1) * P], oTn[:, q * P:(q + 1) * P], wo_sb[:], start=True, stop=True)
                        ins.then_inc(pe_y, 1)

            def between(s):
                if s == -1:
                    pe.wait_ge(ld_w, 16 * NW)
                    pe.wait_ge(dve_const, 1)
                    tn.matmul(m0[:, 0:D], bv_wide[:], wo_sb[:], start=True, stop=True).then_inc(pe_bias, 1)

            EXPERT_STEPS = (4, 6, 8, 10)
            pe.wait_ge(pool_const, 8)
            over_slots(pe.Fori, slot, between)


def kernel(L0_attn_x, L0_attn_Wq, L0_attn_bq, L0_attn_Wk, L0_attn_bk, L0_attn_Wv, L0_attn_bv,
           L0_attn_Wo, L0_attn_bo, L0_ffn_gate_w, L0_ffn_We):
    import numpy as np
    import concourse.bacc as bacc
    from concourse.bass_utils import run_bass_kernel_spmd

    def by_feature(w):
        w = np.asarray(w)
        return np.swapaxes(w.reshape((H, HD) + w.shape[1:]), 0, 1).reshape(w.shape)

    host = {
        "x": np.asarray(L0_attn_x).reshape(NSEQ * S, D),
        "wq": by_feature(L0_attn_Wq).T, "wk": by_feature(L0_attn_Wk).T,
        "bq": by_feature(L0_attn_bq), "bk": by_feature(L0_attn_bk),
        "wv": np.asarray(L0_attn_Wv).T, "bv": np.asarray(L0_attn_bv),
        "wo": np.asarray(L0_attn_Wo).T, "bo": np.asarray(L0_attn_bo),
        "gate": np.asarray(L0_ffn_gate_w).T, "we": np.asarray(L0_ffn_We),
    }
    nc = bacc.Bacc("TRN2", target_bir_lowering=False, num_devices=1)
    arrays, args = {}, {}
    for name, a in host.items():
        arrays[f"in_{name}"] = np.ascontiguousarray(a)
        args[name] = nc.dram_tensor(f"in_{name}", a.shape, FP32, kind="ExternalInput").ap()
    out = nc.dram_tensor("out", (NSEQ * S, D), FP32, kind="ExternalOutput").ap()
    bass_block(nc, out=out, **args)
    r = run_bass_kernel_spmd(nc, [arrays], core_ids=[0])
    return r.results[0]["out"].reshape(NSEQ, S, D)
```
